# Optimizing a Trainium2 kernel written in Bass

```python
import numpy as np
import jax
import jax.numpy as jnp

def _softmax(x, axis=-1):
    return jax.nn.softmax(x, axis=axis)
def _gelu(x):
    return jax.nn.gelu(x, approximate=True)
def _silu(x):
    return jax.nn.silu(x)
def _sigmoid(x):
    return jax.nn.sigmoid(x)
def _layernorm(x, axis=-1, eps=1e-5):
    m = jnp.mean(x, axis=axis, keepdims=True)
    v = jnp.var(x, axis=axis, keepdims=True)
    return (x - m) / jnp.sqrt(v + eps)
def _scatter_add(tgt, idx, src, axis=0):
    return tgt.at[idx].add(src)
def _segment_sum(src, seg, n):
    return jax.ops.segment_sum(src, seg, n)

kernel_name = 'mk_adj_preln_d1_adj_128_13d0f3'

def setup_inputs(seed: int = 0):
    np.random.seed(seed)
    _w = jnp.asarray
    def _rec_inputs():
        import jax
        import jax.numpy as jnp
        _gk = jax.random.key(seed)
        x = -0.003407 + 1.001 * jax.random.normal(jax.random.fold_in(_gk, 1), (4096, 128), jnp.float32)
        _w = (1.0 + jnp.arange(4096, dtype=jnp.float32)) ** -0.5
        _w = _w / _w.mean()
        _pij = jnp.clip(0.00195312 * _w[:, None] * _w[None, :], 0.0, 1.0)
        _a = jax.random.uniform(jax.random.fold_in(_gk, 2), (4096, 4096)) < _pij
        _a = jnp.logical_or(_a, jnp.swapaxes(_a, -1, -2))
        _a = jnp.logical_or(_a, jnp.eye(4096, dtype=bool))
        _af = _a.astype(jnp.float32)
        _af = _af * jax.random.uniform(jax.random.fold_in(_gk, 3), (4096, 4096), jnp.float32, 0.05, 1)
        adj = _af
        return x, adj
    x, adj = _rec_inputs()
    def _L0_gnn_setup():
        import jax, jax.numpy as jnp
        import numpy as np
        LN_EPS = 1e-05
        key = jax.random.key(seed)
        ks = jax.random.split(key, 6)
        N, D = (1024, 128)
        return {'node_feats': jax.random.normal(ks[0], (N, D), dtype=jnp.float32), 'adj': jax.random.uniform(ks[1], (N, N), dtype=jnp.float32), 'msg_w': jax.random.normal(ks[2], (D, 2 * D), dtype=jnp.float32) * 0.05, 'msg_b': jax.random.normal(ks[3], (D,), dtype=jnp.float32) * 0.05, 'upd_w': jax.random.normal(ks[4], (D, 2 * D), dtype=jnp.float32) * 0.05, 'upd_b': jax.random.normal(ks[5], (D,), dtype=jnp.float32) * 0.05, 'ln_w': jnp.ones((D,), dtype=jnp.float32), 'ln_b': jnp.zeros((D,), dtype=jnp.float32)}
    _L0_gnn_all = _L0_gnn_setup()
    _L0_gnn_in = {k: v for k, v in _L0_gnn_all.items() if k in ('msg_w', 'msg_b', 'upd_w', 'upd_b', 'ln_w', 'ln_b', )}
    del _L0_gnn_all

    return {
        "x": x,
        "adj": adj,
        "L0_gnn_msg_w": _L0_gnn_in["msg_w"],
        "L0_gnn_msg_b": _L0_gnn_in["msg_b"],
        "L0_gnn_upd_w": _L0_gnn_in["upd_w"],
        "L0_gnn_upd_b": _L0_gnn_in["upd_b"],
        "L0_gnn_ln_w": _L0_gnn_in["ln_w"],
        "L0_gnn_ln_b": _L0_gnn_in["ln_b"],
    }

def reference(x, adj, L0_gnn_msg_w, L0_gnn_msg_b, L0_gnn_upd_w, L0_gnn_upd_b, L0_gnn_ln_w, L0_gnn_ln_b):
    import jax
    import jax.numpy as jnp
    def _L0_gnn_ref(node_feats, adj, msg_w, msg_b, upd_w, upd_b, ln_w, ln_b):
        import jax, jax.numpy as jnp
        import numpy as np
        LN_EPS = 1e-05
        D = node_feats.shape[-1]
        s = node_feats @ msg_w[:, :D].T
        d = node_feats @ msg_w[:, D:].T
        messages = jax.nn.gelu(s[:, None, :] + d[None, :, :] + msg_b, approximate=False)
        aggregated = jnp.einsum('ijd,ij->id', messages, adj)
        combined = jnp.concatenate([node_feats, aggregated], axis=-1)
        new_feats = combined @ upd_w.T + upd_b
        h = jax.nn.gelu(new_feats, approximate=False) + node_feats
        mu = jnp.mean(h, axis=-1, keepdims=True)
        var = jnp.var(h, axis=-1, keepdims=True)
        return (h - mu) / jnp.sqrt(var + LN_EPS) * ln_w + ln_b

    h = jnp.maximum(_layernorm(x, axis=-1), 0.0)
    x = x + _L0_gnn_ref(h, adj, L0_gnn_msg_w, L0_gnn_msg_b, L0_gnn_upd_w, L0_gnn_upd_b, L0_gnn_ln_w, L0_gnn_ln_b)
    return x


_drawn_inputs = setup_inputs


def setup_inputs(seed=0):
    import zlib

    import numpy as np

    out = dict(_drawn_inputs(seed))
    spreads = {'L0_gnn_ln_w': (1.0, 0.2), 'L0_gnn_ln_b': (0.0, 0.1)}
    factors = {}
    for name, (base, spread) in spreads.items():
        noise = np.random.default_rng([zlib.crc32(name.encode()), seed]).standard_normal(out[name].shape)
        drawn = base * np.exp(spread * noise) if base else spread * noise
        out[name] = jnp.asarray(drawn.astype(out[name].dtype))
    for name, factor in factors.items():
        out[name] = (out[name] * factor).astype(out[name].dtype)
    return out
```

```python
import concourse.bass as bass
from concourse import mybir
from contextlib import ExitStack


def gnn_sparse_rows_kernel(nc, x, adj, msg_w, msg_b, upd_w, upd_b, ln_w, ln_b, out):
    fp32, bf16 = mybir.dt.float32, mybir.dt.bfloat16
    u32, i32 = mybir.dt.uint32, mybir.dt.int32
    ALU = mybir.AluOpType
    ACT = mybir.ActivationFunctionType
    AX_X = mybir.AxisListType.X
    ds = bass.ds

    N, D = x.shape
    P = 128
    assert D == P and N % (4 * P) == 0 and N <= 4096
    T = N // P
    PAIRS = T // 2
    Q = T // 4
    QD = 4 * D
    SEG = 16
    CAND = 8 * SEG
    SLOTS = 64
    G = 4
    NG = SLOTS // G
    RANKS = SLOTS // 8
    EPS = 1e-5
    VALID = 0x20000000
    HALF = 0xFFFF
    FRONT = 5
    STEPS = FRONT + 2 * RANKS + 1

    table = nc.dram_tensor("d_table", (N, D), fp32)

    ctx = ExitStack()
    with ctx:
        def sb(name, shape, dt=fp32):
            return ctx.enter_context(nc.sbuf_tensor(name, shape, dt))

        def bank(name):
            return ctx.enter_context(nc.psum_tensor(name, [P, 512], fp32))

        def sem(name):
            return ctx.enter_context(nc.semaphore(name))

        w_sT = sb("w_sT", [P, D])
        w_dT = sb("w_dT", [P, D])
        w_hT = sb("w_hT", [P, D])
        w_aT = sb("w_aT", [P, D])
        msgb_col = sb("msgb_col", [P, 1])
        msgb_row = sb("msgb_row", [P, D])
        updb_col = sb("updb_col", [P, 1])
        lnw_row = sb("lnw_row", [P, D])
        lnb_row = sb("lnb_row", [P, D])
        ident = sb("ident", [P, P])
        numbered = sb("numbered", [P, P])
        zeros = sb("zeros", [1, P])
        seg_code = sb("seg_code", [P, CAND], i32)
        iota_c = sb("iota_c", [P, CAND], i32)
        h = sb("h", [P, N])
        hT = sb("hT", [P, N + P])
        dT = sb("dT", [P, N])
        sT = sb("sT", [P, N])
        aggT = sb("aggT", [P, N])
        stats6 = sb("stats6", [P, T, 6])
        mean_var = sb("mean_var", [P, T, 2])
        std = sb("std", [P, T])
        rstd = sb("rstd", [P, T])
        shift = sb("shift", [P, T])
        adj_sb = sb("adj_sb", [P, 2, N])
        below = sb("below", [P, N], mybir.dt.uint8)
        neg = sb("neg", [P, 2])
        vals = sb("vals", [P, CAND])
        cols = sb("cols", [P, CAND], u32)
        used = sb("used", [P, CAND])
        seg_full = sb("seg_full", [P, 1])
        n_used = sb("n_used", [P, 1])
        why1 = sb("why1", [P, 1])
        why2 = sb("why2", [P, 1])
        row_stat = sb("row_stat", [P, 2])
        row_ok = sb("row_ok", [P, 1])
        kept = sb("kept", [P, CAND])
        code = sb("code", [P, CAND], u32)
        code_kept = sb("code_kept", [P, CAND], u32)
        key_hi = sb("key_hi", [P, CAND], u32)
        key_lo = sb("key_lo", [P, CAND], u32)
        sort_hi = sb("sort_hi", [P, SLOTS], u32)
        sort_lo = sb("sort_lo", [P, SLOTS], u32)
        val_hi = sb("val_hi", [P, SLOTS], u32)
        idx = sb("idx", [P, 2, SLOTS], i32)
        val = sb("val", [P, 2, SLOTS], u32)
        longest = sb("longest", [1, 2], i32)
        dense_key = sb("dense_key", [1, N + P], bf16)
        ones = sb("ones", [P, 1])
        dense_n = sb("dense_n", [1, T + 1], i32)
        tile_key = sb("tile_key", [1, P])
        key8 = sb("key8", [1, 8])
        key8_i = sb("key8_i", [1, 8], i32)
        row8_i = sb("row8_i", [1, 8], i32)
        dense_sum = sb("dense_sum", [P, 8])
        h_now = sb("h_now", [P, 2, P])
        new_T = sb("new_T", [P, QD])
        slot = sb("slot", [P, 2, SLOTS, D])

        x_sb = slot[:, 0, 0:T, :].rearrange("p t d -> p (t d)")
        msg_sb = slot[:, 0, T:T + 2, :].rearrange("p t d -> p (t d)")
        upd_sb = slot[:, 0, T + 2:T + 4, :].rearrange("p t d -> p (t d)")
        d_rows = slot[:, 1, 0:T, :].rearrange("p t d -> p (t d)")
        f_sb = slot[:, 0, 0:T, :].rearrange("p t d -> p (t d)")
        g_row = [slot[:, b, :, :].rearrange("p s d -> p (s d)")[:, 0:N] for b in range(2)]
        x_end = slot[:, 1, 0:T, :].rearrange("p t d -> p (t d)")

        z_ps = [bank("z0"), bank("z1")]
        agg_ps = [bank("agg0"), bank("agg1")]
        stat_ps = bank("stat_ps")
        work_ps = [bank("work0"), bank("work1"), bank("work2")]

        s_w = sem("weights_loaded")
        s_rows = sem("bias_rows_loaded")
        s_x = sem("x_loaded")
        s_x2 = sem("x_loaded_again")
        s_const = sem("constants_made")
        s_cdve = sem("dve_constant_step")
        s_wT = sem("weights_transposed")
        s_wTc = sem("weights_copied")
        s_ln = sem("layernorm_step")
        s_std = sem("std_ready")
        s_h = sem("h_ready")
        s_hTp = sem("h_transposed")
        s_hT = sem("hT_copied")
        s_dr = sem("d_rows_ready")
        s_drc = sem("d_rows_copied")
        s_dT = sem("dT_ready")
        s_dTc = sem("dT_copied")
        s_sT = sem("sT_ready")
        s_sTc = sem("sT_copied")
        s_tab = sem("d_table_stored")
        s_adj = [sem(f"adj_loaded{b}") for b in range(2)]
        s_neg = sem("negatives_checked")
        s_val = sem("candidates_found")
        s_col = sem("columns_found")
        s_step = sem("extraction_step")
        s_stat = sem("row_stats_ready")
        s_statT = sem("row_stats_on_one_partition")
        s_cnt = sem("longest_ready")
        s_idx = sem("list_columns_ready")
        s_lst = sem("list_values_ready")
        s_iss = sem("gathers_issued")
        s_gat = [[sem(f"gathered{b}_{g}") for g in range(NG)] for b in range(2)]
        s_z = sem("z_ready")
        s_gelu = sem("gelu_done")
        s_hnow = sem("h_now_copied")
        s_newT = sem("update_transposed")
        s_prod = sem("products_ready")
        s_agg = sem("agg_summed")
        s_aggc = sem("agg_copied")
        s_dn = sem("dense_counts_ready")
        s_dstep = sem("dense_list_step")
        s_dcp = sem("dense_keys_copied")
        s_dco = sem("dense_columns_copied")
        s_hadd = sem("h_added")
        s_xb = sem("x_plus_bias_ready")
        s_dlist = sem("dense_rows_listed")
        s_drow = [sem(f"dense_adj_loaded{b}") for b in range(2)]
        s_dg = sem("dense_gelu_done")
        s_dsum = sem("dense_sum_done")
        s_end = sem("dense_path_done")
        s_up = sem("update_ready")
        s_upg = sem("update_gelu_done")
        s_fin = sem("final_step")
        s_nrm = sem("normalized")
        s_scl = sem("scaled")
        s_y = sem("output_ready")
        s_out = sem("output_stored")

        s_held = {e: sem(f"held_{e}") for e in ("sp", "pool", "act", "pe", "dve")}

        block = ctx.enter_context(nc.Block())

        def holder(eng, held):
            def hold(semaphore, value):
                eng.wait_ge(semaphore, value)
                eng.sem_inc(held, 1)
            return hold

        rows_of = lambda t: adj[ds(t * P, P), :]

        @block.sync
        def _(sp):
            hold = holder(sp, s_held["sp"])
            sp.dma_start(x_sb.rearrange("p (t d) -> p t d", d=D),
                         x.rearrange("(t p) d -> p t d", p=P)).then_inc(s_x, 16)
            sp.dma_start(msg_sb, msg_w).then_inc(s_w, 16)
            sp.dma_start(upd_sb, upd_w).then_inc(s_w, 16)
            for dst, src in ((msgb_row, msg_b), (lnw_row, ln_w), (lnb_row, ln_b)):
                sp.dma_start(dst[:], src.partition_broadcast(P)).then_inc(s_rows, 16)
            sp.dma_start(updb_col[:], upd_b.rearrange("(n a) -> n a", a=1)).then_inc(s_rows, 16)
            sp.dma_start(msgb_col[:], msg_b.rearrange("(n a) -> n a", a=1)).then_inc(s_rows, 16)
            with sp.Fori(0, PAIRS) as k:
                for b in range(2):
                    sp.wait_ge(s_col, 2 * k + b + 1)
                    sp.wait_ge(s_neg, 2 * k + b + 1)
                    sp.dma_start(adj_sb[:, b, :], rows_of(2 * k + b)).then_inc(s_adj[b], 16)
            sp.wait_ge(s_dn, 1)
            rounds = sp.alloc_register("sp_rounds")
            sp.reg_mov(rounds, 0)
            with sp.Fori(0, T) as t:
                n = sp.value_load(dense_n[0:1, ds(t, 1)], min_val=0, max_val=P)
                with sp.If(n > 0):
                    with sp.Fori(0, P // 8) as r:
                        with sp.If(n > r * 8):
                            c = sp.snap(rounds, min_val=0, max_val=N // 8)
                            hold(s_dlist, c + 1)
                            for j in range(8):
                                i = sp.value_load(row8_i[0:1, j:j + 1], min_val=0, max_val=P - 1)
                                sp.wait_ge(s_dsum, c * 8 + j + 1)
                                sp.dma_start(adj_sb[:, j % 2, :],
                                             adj[ds(t * P + i, 1), :].partition_broadcast(P))\
                                    .then_inc(s_drow[j % 2], 16)
                            sp.reg_add(rounds, rounds, 1)
            sp.wait_ge(s_end, 1)
            sp.dma_start(x_end.rearrange("p (t d) -> p t d", d=D),
                         x.rearrange("(t p) d -> p t d", p=P)).then_inc(s_x2, 16)
            with sp.Fori(0, Q) as q:
                sp.wait_ge(s_y, q + 1)
                sp.dma_start(out.rearrange("(t p) d -> p t d", p=P)[:, ds(4 * q, 4), :],
                             f_sb.rearrange("p (t d) -> p t d", d=D)[:, ds(4 * q, 4), :])\
                    .then_inc(s_out, 16)
            sp.wait_ge(s_out, 16 * Q)

        @block.gpsimd
        def _(pool):
            hold = holder(pool, s_held["pool"])
            pool.sem_inc(s_iss, 2)
            pool.memset(ident[:], 0.0).then_inc(s_const, 1)
            pool.memset(numbered[:], 0.0).then_inc(s_const, 1)
            pool.iota(iota_c[:], pattern=[[1, SEG], [0, 8]], base=0, channel_multiplier=0).then_inc(s_const, 1)
            pool.wait_ge(s_const, 3)
            pool.affine_select(out=ident[:], in_=ident[:], compare_op=ALU.not_equal, fill=1.0,
                               base=0, pattern=[[-1, P]], channel_multiplier=1).then_inc(s_const, 1)
            pool.iota(sort_hi[:].bitcast(i32)[:, 0:1], pattern=[[0, 1]], base=1, channel_multiplier=1).then_inc(s_const, 1)
            with pool.Fori(0, Q) as q:
                pool.wait_ge(s_drc, q + 1)
                pool.dma_start(table.ap().rearrange("(t p) d -> p t d", p=P)[:, ds(4 * q, 4), :],
                               d_rows.rearrange("p (t d) -> p t d", d=D)[:, ds(4 * q, 4), :])\
                    .then_inc(s_tab, 16)
            pool.wait_ge(s_tab, 16 * Q)

            def gathers(k, b):
                t = 2 * k + b
                pool.wait_ge(s_idx, t + 1)
                hold(s_agg, t + 1)
                n = pool.value_load(longest[0:1, b:b + 1], min_val=0, max_val=SLOTS)
                for g0 in range(0, NG, 4):
                    with pool.If(n > G * g0):
                        for g in range(g0, g0 + 4):
                            with pool.If(n > G * g):
                                for s in range(G * g, G * g + G):
                                    pool.indirect_dma_start(
                                        out=slot[:, b, s, :], out_offset=None, in_=table.ap(),
                                        in_offset=bass.IndirectOffsetOnAxis(ap=idx[:, b, s:s + 1], axis=0))\
                                        .then_inc(s_gat[b][g], 16)
                        pool.nop()
                pool.sem_inc(s_iss, 1)

            with pool.Fori(0, PAIRS) as k:
                gathers(k, 0)
                gathers(k, 1)

        @block.scalar
        def _(act):
            hold = holder(act, s_held["act"])
            act.sem_inc(s_neg, 2)
            act.sem_inc(s_gelu, 2)
            act.sem_inc(s_aggc, 2)
            act.wait_ge(s_ln, 2)
            act.activation(std[:], mean_var[:, :, 1], ACT.Sqrt).then_inc(s_std, 1)
            act.wait_ge(s_ln, 4)
            act.wait_ge(s_x, 16)
            with act.Fori(0, Q) as q:
                for j in range(4):
                    at = ds((4 * q + j) * D, D)
                    last = act.activation(h[:, at], x_sb[:, at], ACT.Relu,
                                          bias=shift[:, ds(4 * q + j, 1)], scale=rstd[:, ds(4 * q + j, 1)])
                last.then_inc(s_h, 1)
            act.wait_ge(s_rows, 80)
            with act.Fori(0, Q) as q:
                act.wait_ge(s_dT, q + 1)
                act.activation(dT[:, ds(q * QD, QD)], work_ps[1][:], ACT.Identity,
                               bias=msgb_col[:, 0:1]).then_inc(s_dTc, 1)
                act.wait_ge(s_sT, q + 1)
                act.activation(sT[:, ds(q * QD, QD)], work_ps[2][:], ACT.Copy).then_inc(s_sTc, 1)

            def negatives(u, k, b):
                act.activation(h_now[:, b, :], hT[:, ds(u * P, P)], ACT.Copy).then_inc(s_hnow, 1)
                act.wait_ge(s_adj[b], 16 * (k + 1))
                act.wait_ge(s_step, STEPS * u)
                act.wait_ge(s_neg, u + 2)
                act.activation(below[:], adj_sb[:, b, :], ACT.Relu, scale=-1.0,
                               accum_out=neg[:, b:b + 1]).then_inc(s_neg, 1)

            def gelus(t, b):
                hold(s_cnt, t + 1)
                n = act.value_load(longest[0:1, b:b + 1], min_val=0, max_val=SLOTS)
                for g0 in range(0, NG, 4):
                    with act.If(n > G * g0):
                        for g in range(g0, g0 + 4):
                            with act.If(n > G * g):
                                act.wait_ge(s_z, t * NG + g + 1)
                                act.activation(slot[:, b, G * g:G * g + G, :].rearrange("p s d -> p (s d)"),
                                               z_ps[g % 2][:], ACT.Gelu).then_inc(s_gelu, 1)
                            with act.Else():
                                act.wait_ge(s_gelu, t * NG + g + 2)
                                act.sem_inc(s_gelu, 1)
                        act.nop()
                    with act.Else():
                        act.wait_ge(s_gelu, t * NG + g0 + 2)
                        act.sem_inc(s_gelu, 4)
                act.wait_ge(s_agg, t + 3)
                act.activation(aggT[:, ds(t * P, P)], agg_ps[b][:, 0:P], ACT.Copy).then_inc(s_aggc, 1)

            negatives(0, 0, 0)
            with act.Fori(0, PAIRS) as k:
                negatives(2 * k + 1, k, 1)
                gelus(2 * k, 0)
                with act.If(k < PAIRS - 1):
                    negatives(2 * k + 2, k + 1, 0)
                gelus(2 * k + 1, 1)

            act.wait_ge(s_dn, 1)
            rounds = act.alloc_register("act_rounds")
            act.reg_mov(rounds, 0)
            with act.Fori(0, T) as t:
                n = act.value_load(dense_n[0:1, ds(t, 1)], min_val=0, max_val=P)
                with act.If(n > 0):
                    with act.Fori(0, P // 8) as r:
                        with act.If(n > r * 8):
                            c = act.snap(rounds, min_val=0, max_val=N // 8)
                            hold(s_dlist, c + 1)
                            for j in range(8):
                                i = act.value_load(row8_i[0:1, j:j + 1], min_val=0, max_val=P - 1)
                                act.wait_ge(s_dsum, c * 8 + j + 1)
                                act.activation(g_row[j % 2], dT[:], ACT.Gelu,
                                               bias=sT[:, ds(t * P + i, 1)]).then_inc(s_dg, 1)
                            act.reg_add(rounds, rounds, 1)
            with act.Fori(0, Q) as q:
                act.wait_ge(s_up, q + 1)
                act.wait_ge(s_hadd, q + 1)
                act.activation(new_T[:], work_ps[0][:], ACT.Gelu, bias=updb_col[:, 0:1]).then_inc(s_upg, 1)
            act.wait_ge(s_fin, 2)
            act.activation(std[:], mean_var[:, :, 1], ACT.Sqrt).then_inc(s_std, 1)
            act.wait_ge(s_fin, 4)
            with act.Fori(0, Q) as q:
                for j in range(4):
                    at = ds((4 * q + j) * D, D)
                    last = act.activation(f_sb[:, at], f_sb[:, at], ACT.Identity,
                                          bias=shift[:, ds(4 * q + j, 1)], scale=rstd[:, ds(4 * q + j, 1)])
                last.then_inc(s_nrm, 1)

        @block.tensor
        def _(pe):
            hold = holder(pe, s_held["pe"])
            pe.sem_inc(s_agg, 2)
            pe.wait_ge(s_w, 32)
            pe.wait_ge(s_const, 4)
            for j, (w, half) in enumerate(((msg_sb, 0), (msg_sb, 1), (upd_sb, 0), (upd_sb, 1))):
                last = pe.transpose(z_ps[0][:, j * D:(j + 1) * D], w[:, half * D:(half + 1) * D], ident[:])
            last.then_inc(s_wT, 1)
            pe.wait_ge(s_wTc, 1)
            for q in range(Q):
                pe.wait_ge(s_h, q + 1)
                for j in range(4):
                    last = pe.transpose(z_ps[1][:, j * P:(j + 1) * P], h[:, (4 * q + j) * D:(4 * q + j + 1) * D],
                                        ident[:])
                last.then_inc(s_hTp, 1)
                pe.wait_ge(s_hT, q + 1)
                if q:
                    pe.wait_ge(s_drc, q)
                for j in range(4):
                    last = pe.matmul(work_ps[0][:, j * D:(j + 1) * D], hT[:, (4 * q + j) * P:(4 * q + j + 1) * P], w_dT[:],
                                     start=True, stop=True)
                last.then_inc(s_dr, 1)
                if q:
                    pe.wait_ge(s_dTc, q)
                    pe.wait_ge(s_sTc, q)
                pe.matmul(work_ps[1][:], w_dT[:], hT[:, q * QD:(q + 1) * QD], start=True, stop=True).then_inc(s_dT, 1)
                pe.matmul(work_ps[2][:], w_sT[:], hT[:, q * QD:(q + 1) * QD], start=True, stop=True).then_inc(s_sT, 1)

            def stats(u):
                pe.wait_ge(s_stat, u + 1)
                pe.wait_ge(s_cnt, u)
                pe.matmul(stat_ps[0:1, 0:P], row_stat[:, 0:1], ident[:], start=True, stop=True)
                pe.matmul(stat_ps[0:1, P:2 * P], row_stat[:, 1:2], numbered[:], start=True, stop=True)
                pe.matmul(stat_ps[0:1, 2 * P:2 * P + 1], row_stat[:, 1:2], ones[:], start=True, stop=True)\
                    .then_inc(s_statT, 1)

            w_s4 = w_sT[:].unsqueeze(1).to_broadcast([P, G, D])

            def tile_sums(t, k, b):
                hold(s_cnt, t + 1)
                n = pe.value_load(longest[0:1, b:b + 1], min_val=0, max_val=SLOTS)
                pe.wait_ge(s_aggc, t + 1)
                pe.matmul(agg_ps[b][:, 0:P], zeros[:], zeros[:], start=True, stop=False)
                pe.wait_ge(s_hnow, t + 1)

                def z_of(g):
                    pe.wait_ge(s_gat[b][g], pe.snap(due[b][g], min_val=16 * G, max_val=16 * G * PAIRS))
                    pe.reg_add(due[b][g], due[b][g], 16 * G)
                    pe.wait_ge(s_gelu, t * NG + g + 1)
                    pe.matmul(z_ps[g % 2][:], ident[:],
                              slot[:, b, G * g:G * g + G, :].rearrange("p s d -> p (s d)"), start=True, stop=False)
                    pe.matmul(z_ps[g % 2][:].rearrange("p (s d) -> p s d", s=G), h_now[:, b, :], w_s4,
                              start=False, stop=True).then_inc(s_z, 1)

                def sum_of(g):
                    pe.wait_ge(s_prod, t * NG + g + 1)
                    for s in range(G * g, G * g + G):
                        pe.matmul(agg_ps[b][:, 0:P], slot[:, b, s, :], ident[:], start=False, stop=False)

                for g0 in range(0, NG, 4):
                    with pe.If(n > G * g0):
                        for g in range(g0, g0 + 4):
                            with pe.If(n > G * g):
                                z_of(g)
                            with pe.Else():
                                pe.wait_ge(s_z, t * NG + g)
                                pe.sem_inc(s_z, 1)
                        for g in range(g0, g0 + 4):
                            with pe.If(n > G * g):
                                sum_of(g)
                        pe.nop()
                    with pe.Else():
                        pe.wait_ge(s_z, t * NG + g0)
                        pe.sem_inc(s_z, 4)
                pe.matmul(agg_ps[b][:, 0:P], zeros[:], zeros[:], start=False, stop=True).then_inc(s_agg, 1)

            due = [[pe.alloc_register(f"due{b}_{g}") for g in range(NG)] for b in range(2)]
            for b in range(2):
                for g in range(NG):
                    pe.reg_mov(due[b][g], 16 * G)
            stats(0)
            with pe.Fori(0, PAIRS) as k:
                stats(2 * k + 1)
                tile_sums(2 * k, k, 0)
                with pe.If(k < PAIRS - 1):
                    stats(2 * k + 2)
                tile_sums(2 * k + 1, k, 1)

            pe.wait_ge(s_end, 1)
            with pe.Fori(0, Q) as q:
                pe.matmul(work_ps[0][:], w_hT[:], hT[:, ds(q * QD, QD)], start=True, stop=False)
                pe.matmul(work_ps[0][:], w_aT[:], aggT[:, ds(q * QD, QD)], start=False, stop=True).then_inc(s_up, 1)
                pe.wait_ge(s_upg, q + 1)
                pe.wait_ge(s_hadd, q + 1)
                for j in range(4):
                    last = pe.transpose(work_ps[1][:, j * P:(j + 1) * P], new_T[:, j * P:(j + 1) * P], ident[:])
                last.then_inc(s_newT, 1)

        @block.vector
        def _(dve):
            hold = holder(dve, s_held["dve"])
            dve.sem_inc(s_col, 2)
            dve.sem_inc(s_dco, 1)
            dve.sem_inc(s_dsum, 2)
            dve.memset(zeros[:], 0.0)
            dve.memset(ones[:], 1.0)
            dve.memset(sort_lo[:], 0)
            dve.wait_ge(s_const, 5)
            dve.tensor_scalar(seg_code[:], iota_c[:], 16, VALID, ALU.logical_shift_left, ALU.bitwise_or)
            dve.tensor_copy(why1[:], sort_hi[:].bitcast(i32)[:, 0:1]).then_inc(s_cdve, 1)
            dve.wait_ge(s_cdve, 1)
            dve.tensor_scalar(numbered[:], ident[:], why1[:, 0:1], None, ALU.mult)
            dve.memset(sort_hi[:], 0).then_inc(s_cdve, 1)

            def norm_stats(src, s_in, first, step):
                for t in range(T):
                    last = dve.bn_stats(stats6[:, t, :], src[:, t * D:(t + 1) * D])
                last.then_inc(step, 1)
                dve.wait_ge(step, 1)
                for t in range(T):
                    last = dve.bn_aggr(mean_var[:, t, :], stats6[:, t, :])
                last.then_inc(s_cdve, 1)
                dve.wait_ge(s_cdve, first)
                dve.tensor_scalar(mean_var[:, :, 1], mean_var[:, :, 1], EPS, None, ALU.add).then_inc(step, 1)
                dve.wait_ge(s_std, s_in)
                dve.reciprocal(rstd[:], std[:]).then_inc(step, 1)
                dve.wait_ge(step, 3)
                dve.scalar_tensor_tensor(shift[:], mean_var[:, :, 0], -1.0, rstd[:], ALU.mult, ALU.mult)\
                    .then_inc(step, 1)

            dve.wait_ge(s_x, 16)
            norm_stats(x_sb, 1, 3, s_ln)
            dve.wait_ge(s_wT, 1)
            for j, w in enumerate((w_sT, w_dT, w_hT, w_aT)):
                last = dve.tensor_copy(w[:], z_ps[0][:, j * D:(j + 1) * D])
            last.then_inc(s_wTc, 1)
            dve.wait_ge(s_rows, 80)
            with dve.Fori(0, Q) as q:
                dve.wait_ge(s_hTp, q + 1)
                dve.tensor_copy(hT[:, ds(q * QD, QD)], z_ps[1][:]).then_inc(s_hT, 1)
                dve.wait_ge(s_dr, q + 1)
                dve.tensor_tensor(d_rows[:, ds(q * QD, QD)].rearrange("p (t d) -> p t d", d=D),
                                  work_ps[0][:].rearrange("p (t d) -> p t d", d=D),
                                  msgb_row[:].unsqueeze(1).to_broadcast([P, 4, D]), ALU.add).then_inc(s_drc, 1)

            def extract(u, k, b):
                done = lambda n: hold(s_step, STEPS * u + n)
                hold(s_adj[b], 16 * (k + 1))
                seg = adj_sb[:, b, :].rearrange("p (c s) -> p s c", s=SEG)
                for s in range(SEG):
                    last = dve.max(vals[:, 8 * s:8 * s + 8], seg[:, s, :])
                last.then_inc(s_val, 1)
                hold(s_val, u + 1)
                for s in range(SEG):
                    last = dve.max_index(cols[:, 8 * s:8 * s + 8], vals[:, 8 * s:8 * s + 8], seg[:, s, :])
                last.then_inc(s_col, 1)
                dve.tensor_reduce(seg_full[:], vals[:].rearrange("p (s e) -> p s e", e=8)[:, :, 7], AX_X, ALU.max)
                dve.tensor_scalar(used[:], vals[:], 0.0, None, ALU.not_equal, ALU.add, accum_out=n_used[:])\
                    .then_inc(s_step, 1)
                done(1)
                dve.wait_ge(s_neg, u + 3)
                dve.scalar_tensor_tensor(why1[:], seg_full[:], 0.0, neg[:, b:b + 1], ALU.not_equal, ALU.add)\
                    .then_inc(s_step, 1)
                dve.wait_ge(s_col, u + 3)
                dve.scalar_tensor_tensor(code[:], cols[:], 20, seg_code[:].bitcast(u32),
                                         ALU.logical_shift_left, ALU.bitwise_or)
                done(2)
                dve.scalar_tensor_tensor(why2[:], n_used[:], float(SLOTS), why1[:], ALU.is_gt, ALU.add)\
                    .then_inc(s_step, 1)
                done(3)
                dve.wait_ge(s_statT, u)
                dve.scalar_tensor_tensor(row_stat[:, 0:1], why2[:], 0.0, n_used[:], ALU.is_equal, ALU.mult)
                dve.tensor_scalar(row_ok[:], why2[:], 0.0, None, ALU.is_equal)
                dve.tensor_scalar(row_stat[:, 1:2], why2[:], 0.0, None, ALU.not_equal).then_inc(s_stat, 1)
                dve.wait_ge(s_stat, u + 1)
                dve.tensor_scalar(kept[:], vals[:], row_ok[:, 0:1], None, ALU.mult).then_inc(s_step, 1)
                done(4)
                dve.scalar_tensor_tensor(code_kept[:].bitcast(fp32), kept[:], 0.0, code[:].bitcast(fp32),
                                         ALU.not_equal, ALU.mult).then_inc(s_step, 1)
                done(FRONT)
                dve.scalar_tensor_tensor(key_hi[:], kept[:].bitcast(u32), 16, code_kept[:],
                                         ALU.logical_shift_right, ALU.bitwise_or)
                dve.scalar_tensor_tensor(key_lo[:], kept[:].bitcast(u32), HALF, code_kept[:],
                                         ALU.bitwise_and, ALU.bitwise_or)
                dve.wait_ge(s_statT, u + 1)
                dve.wait_ge(s_iss, u + 1)
                dve.wait_ge(s_aggc, u + 1)
                dve.tensor_reduce(longest[0:1, b:b + 1], stat_ps[0:1, 0:P], AX_X, ALU.max)
                dve.tensor_copy(dense_n[0:1, ds(u, 1)], stat_ps[0:1, 2 * P:2 * P + 1])
                dve.tensor_copy(dense_key[0:1, ds(u * P, P)], stat_ps[0:1, P:2 * P]).then_inc(s_cnt, 1)
                hold(s_cnt, u + 1)
                n = dve.value_load(longest[0:1, b:b + 1], min_val=0, max_val=SLOTS)
                f_hi, f_lo = key_hi[:].bitcast(fp32), key_lo[:].bitcast(fp32)
                t_hi, t_lo = sort_hi[:].bitcast(fp32), sort_lo[:].bitcast(fp32)
                for r in range(RANKS):
                    with dve.If(n > 8 * r):
                        dve.max(t_hi[:, 8 * r:8 * r + 8], f_hi)
                        dve.max(t_lo[:, 8 * r:8 * r + 8], f_lo).then_inc(s_step, 1)
                        done(FRONT + 2 * r + 1)
                        dve.match_replace(f_hi, t_hi[:, 8 * r:8 * r + 8], f_hi, 0.0)
                        dve.match_replace(f_lo, t_lo[:, 8 * r:8 * r + 8], f_lo, 0.0).then_inc(s_step, 1)
                        done(FRONT + 2 * r + 2)
                    with dve.Else():
                        dve.sem_inc(s_step, 2)
                done(FRONT + 2 * RANKS)
                dve.tensor_scalar(idx[:, b, :].bitcast(u32), sort_hi[:], 16, 0xFFF,
                                  ALU.logical_shift_right, ALU.bitwise_and).then_inc(s_idx, 1)
                dve.tensor_scalar(val_hi[:], sort_hi[:], HALF, 16, ALU.bitwise_and, ALU.logical_shift_left)\
                    .then_inc(s_step, 1)
                done(STEPS)
                dve.scalar_tensor_tensor(val[:, b, :], sort_lo[:], HALF, val_hi[:],
                                         ALU.bitwise_and, ALU.bitwise_or).then_inc(s_lst, 1)

            def products(t, b):
                n = dve.value_load(longest[0:1, b:b + 1], min_val=0, max_val=SLOTS)
                hold(s_lst, t + 1)
                for g0 in range(0, NG, 4):
                    with dve.If(n > G * g0):
                        for g in range(g0, g0 + 4):
                            with dve.If(n > G * g):
                                dve.wait_ge(s_gelu, t * NG + g + 3)
                                at = slot[:, b, G * g:G * g + G, :]
                                v = val[:, b, G * g:G * g + G].bitcast(fp32)
                                dve.tensor_tensor(at, at, v.unsqueeze(2).to_broadcast([P, G, D]), ALU.mult)\
                                    .then_inc(s_prod, 1)
                            with dve.Else():
                                dve.wait_ge(s_prod, t * NG + g)
                                dve.sem_inc(s_prod, 1)
                        dve.nop()
                    with dve.Else():
                        dve.wait_ge(s_prod, t * NG + g0)
                        dve.sem_inc(s_prod, 4)

            extract(0, 0, 0)
            with dve.Fori(0, PAIRS) as k:
                extract(2 * k + 1, k, 1)
                products(2 * k, 0)
                with dve.If(k < PAIRS - 1):
                    extract(2 * k + 2, k + 1, 0)
                products(2 * k + 1, 1)

            dve.wait_ge(s_aggc, T + 2)
            dve.sem_inc(s_dn, 1)
            rounds = dve.alloc_register("dve_rounds")
            dve.reg_mov(rounds, 0)
            LIST = 4
            copies = dve.alloc_register("dve_copies")
            dve.reg_mov(copies, 0)
            with dve.Fori(0, T) as t:
                n = dve.value_load(dense_n[0:1, ds(t, 1)], min_val=0, max_val=P)
                with dve.If(n > 0):
                    cc = dve.snap(copies, min_val=0, max_val=T)
                    dve.tensor_copy(tile_key[:], dense_key[0:1, ds(t * P, P)]).then_inc(s_dcp, 1)
                    hold(s_dcp, cc + 1)
                    dve.reg_add(copies, copies, 1)
                    with dve.Fori(0, P // 8) as r:
                        with dve.If(n > r * 8):
                            c = dve.snap(rounds, min_val=0, max_val=N // 8)
                            dve.max(key8[:], tile_key[:]).then_inc(s_dstep, 1)
                            hold(s_dstep, c * 2 + 1)
                            dve.match_replace(tile_key[:], key8[:], tile_key[:], 0.0)
                            dve.tensor_copy(key8_i[:], key8[:])
                            dve.tensor_scalar(row8_i[:], key8[:], -1.0, 0.0, ALU.add, ALU.max).then_inc(s_dlist, 1)
                            dve.wait_ge(s_dlist, c + 1)
                            for j in range(8):
                                dve.wait_ge(s_dg, c * 8 + j + 1)
                                dve.wait_ge(s_drow[j % 2], c * 64 + 16 * (j // 2 + 1))
                                dve.tensor_tensor_reduce(out=g_row[j % 2], in0=g_row[j % 2], in1=adj_sb[:, j % 2, :],
                                                         scale=1.0, scalar=0.0, op0=ALU.mult, op1=ALU.add,
                                                         accum_out=dense_sum[:, j:j + 1]).then_inc(s_dsum, 1)
                            hold(s_dsum, c * 8 + 10)
                            for j in range(8):
                                i = dve.value_load(key8_i[0:1, j:j + 1], min_val=0, max_val=P)
                                with dve.If(i > 0):
                                    row = dve.value_load(row8_i[0:1, j:j + 1], min_val=0, max_val=P - 1)
                                    dve.tensor_copy(aggT[:, ds(t * P + row, 1)], dense_sum[:, j:j + 1])\
                                        .then_inc(s_dco, 1)
                                with dve.Else():
                                    dve.wait_ge(s_dco, c * 8 + j + 1)
                                    dve.sem_inc(s_dco, 1)
                            hold(s_dco, c * 8 + 9)
                            dve.sem_inc(s_dstep, 1)
                            dve.reg_add(rounds, rounds, 1)
            dve.sem_inc(s_hadd, 1)
            dve.sem_inc(s_end, 1)

            row4 = lambda r: r[:].unsqueeze(1).to_broadcast([P, 4, D])
            quad = lambda a, q: a[:, ds(q * QD, QD)].rearrange("p (t d) -> p t d", d=D)
            with dve.Fori(0, Q) as q:
                dve.wait_ge(s_newT, q + 1)
                dve.tensor_tensor(f_sb[:, ds(q * QD, QD)], work_ps[1][:], h[:, ds(q * QD, QD)],
                                  ALU.add).then_inc(s_hadd, 1)
            dve.wait_ge(s_x2, 16)
            with dve.Fori(0, Q) as q:
                dve.tensor_tensor(quad(x_end, q), quad(x_end, q), row4(lnb_row), ALU.add).then_inc(s_xb, 1)
            dve.wait_ge(s_hadd, Q + 1)
            norm_stats(f_sb, 2, 4, s_fin)
            dve.wait_ge(s_xb, Q)
            with dve.Fori(0, Q) as q:
                dve.wait_ge(s_nrm, q + 1)
                dve.tensor_tensor(quad(f_sb, q), quad(f_sb, q), row4(lnw_row), ALU.mult).then_inc(s_scl, 1)
                dve.wait_ge(s_scl, q + 1)
                dve.tensor_tensor(quad(f_sb, q), quad(f_sb, q), quad(x_end, q), ALU.add).then_inc(s_y, 1)


_INS = ["x", "adj", "L0_gnn_msg_w", "L0_gnn_msg_b", "L0_gnn_upd_w", "L0_gnn_upd_b", "L0_gnn_ln_w", "L0_gnn_ln_b"]


def kernel(**inputs):
    import numpy as _np
    import concourse.bacc as _bacc
    from concourse import mybir as _mybir
    from concourse.bass_utils import run_bass_kernel_spmd as _run

    nc = _bacc.Bacc("TRN2", target_bir_lowering=False, num_devices=1)
    arrays, args = {}, []
    for name in _INS:
        a = _np.ascontiguousarray(inputs[name])
        arrays[f"in_{name}"] = a
        args.append(nc.dram_tensor(f"in_{name}", a.shape, _mybir.dt.from_np(a.dtype), kind="ExternalInput").ap())
    shape = arrays["in_x"].shape
    args.append(nc.dram_tensor("out_0", shape, _mybir.dt.float32, kind="ExternalOutput").ap())
    gnn_sparse_rows_kernel(nc, *args)
    r = _run(nc, [arrays], core_ids=[0])
    return r.results[0]["out_0"]
```

```python
import concourse.bass as bass
from concourse import mybir
from contextlib import ExitStack


def gnn_sparse_rows_kernel(nc, x, adj, msg_w, msg_b, upd_w, upd_b, ln_w, ln_b, out):
    fp32, u8 = mybir.dt.float32, mybir.dt.uint8
    u32, i32 = mybir.dt.uint32, mybir.dt.int32
    ALU = mybir.AluOpType
    ACT = mybir.ActivationFunctionType
    AX_X = mybir.AxisListType.X
    ds = bass.ds

    N, D = x.shape
    P = 128
    assert D == P and N % (4 * P) == 0 and N <= 4096
    T = N // P
    PARTS = 8
    RP = P // PARTS
    NT = PARTS + T - 1
    assert NT % 2 == 1 and T >= 8
    PW = N // PARTS
    VP = PARTS // 2
    PAIRS = NT // 2
    Q = T // 4
    QD = 4 * D
    SEG = 16
    CAND = 8 * SEG
    SLOTS = 64
    G = 4
    NG = SLOTS // G
    RANKS = SLOTS // 8
    EPS = 1e-5
    VALID = 0x20000000
    HALF = 0xFFFF
    SURE = 3

    table = nc.dram_tensor("d_table", (N, D), fp32)

    ctx = ExitStack()
    with ctx:
        def sb(name, shape, dt=fp32):
            return ctx.enter_context(nc.sbuf_tensor(name, shape, dt))

        def bank(name):
            return ctx.enter_context(nc.psum_tensor(name, [P, 512], fp32))

        def sem(name):
            return ctx.enter_context(nc.semaphore(name))

        w_sT = sb("w_sT", [P, D])
        w_dT = sb("w_dT", [P, D])
        w_hT = sb("w_hT", [P, D])
        w_aT = sb("w_aT", [P, D])
        msgb_col = sb("msgb_col", [P, 1])
        msgb_row = sb("msgb_row", [P, D])
        updb_col = sb("updb_col", [P, 1])
        lnw_row = sb("lnw_row", [P, D])
        lnb_row = sb("lnb_row", [P, D])
        ident = sb("ident", [P, P])
        same_row = sb("same_row", [P, P])
        number = sb("number", [1, P])
        number_i = sb("number_i", [1, P], i32)
        zeros = sb("zeros", [1, P])
        seg_code = sb("seg_code", [P, CAND], i32)
        part_code = sb("part_code", [P, CAND], i32)
        h = sb("h", [P, N])
        hT = sb("hT", [P, N + P])
        dT = sb("dT", [P, N])
        x_sb = sb("x_sb", [P, N])
        agg_parts = sb("agg_parts", [P, PARTS * P])
        aggT = sb("aggT", [P, N])
        stats6 = sb("stats6", [P, T, 6])
        mean_var = sb("mean_var", [P, T, 2])
        std = sb("std", [P, T])
        rstd = sb("rstd", [P, T])
        shift = sb("shift", [P, T])
        adj_sb = sb("adj_sb", [P, 2, N])
        below = sb("below", [P, N], u8)
        neg = sb("neg", [P, 2])
        vals = sb("vals", [P, 2, CAND])
        cols = sb("cols", [P, CAND], u32)
        used = sb("used", [P, CAND])
        seg_full = sb("seg_full", [P, 1])
        n_used = sb("n_used", [P, 1])
        why1 = sb("why1", [P, 1])
        why2 = sb("why2", [P, 1])
        row_stat = sb("row_stat", [P, 2])
        row_ok = sb("row_ok", [P, 1])
        kept = sb("kept", [P, CAND])
        iota_c, iota_p = kept[:].bitcast(i32), used[:].bitcast(i32)
        code = sb("code", [P, 2, CAND], u32)
        code_kept = sb("code_kept", [P, CAND], u32)
        key_hi = sb("key_hi", [P, CAND], u32)
        key_lo = sb("key_lo", [P, CAND], u32)
        sort_hi = sb("sort_hi", [P, SLOTS], u32)
        sort_lo = sb("sort_lo", [P, SLOTS], u32)
        val_hi = sb("val_hi", [P, SLOTS], u32)
        idx = sb("idx", [P, 2, SLOTS], i32)
        val = sb("val", [P, 2, SLOTS], u32)
        longest = sb("longest", [1, 2], i32)
        dense_flag = sb("dense_flag", [1, NT * P], u8)
        first_flag = sb("first_flag", [1, P], u8)
        dense_n = sb("dense_n", [1, T], i32)
        tile_key = sb("tile_key", [1, P])
        key8 = sb("key8", [1, 8])
        row8_i = sb("row8_i", [1, 8], i32)
        dense_sum = sb("dense_sum", [P, 8])
        s_colm = sb("s_colm", [P, 2])
        h_now = sb("h_now", [P, 2, P])
        new_T = agg_parts[:, 0:QD]
        slot = sb("slot", [P, 2, SLOTS, D])

        msg_sb = slot[:, 0, T:T + 2, :].rearrange("p t d -> p (t d)")
        upd_sb = slot[:, 0, T + 2:T + 4, :].rearrange("p t d -> p (t d)")
        d_rows = slot[:, 1, 0:T, :].rearrange("p t d -> p (t d)")
        f_sb = slot[:, 0, 0:T, :].rearrange("p t d -> p (t d)")
        g_row = [slot[:, b, :, :].rearrange("p s d -> p (s d)")[:, 0:N] for b in range(2)]

        z_ps = [bank("z0"), bank("z1")]
        agg_ps = [bank("agg0"), bank("agg1")]
        stat_ps = bank("stat_ps")
        or_ps = stat_ps[:, 2 * P:2 * P + 1]
        work_ps = [bank("work0"), bank("work1"), bank("work2")]

        s_w = sem("weights_loaded")
        s_rows = sem("bias_rows_loaded")
        s_x = [sem(f"x_loaded{q}") for q in range(Q)]
        s_const = sem("constants_made")
        s_cdve = sem("dve_constant_step")
        s_wT = sem("weights_transposed")
        s_wTc = sem("weights_copied")
        s_ln = sem("layernorm_step")
        s_std = sem("std_ready")
        s_h = sem("h_ready")
        s_hTp = sem("h_transposed")
        s_hT = sem("hT_copied")
        s_dr = sem("d_rows_ready")
        s_drc = sem("d_rows_copied")
        s_dT = sem("dT_ready")
        s_dTc = sem("dT_copied")
        s_tab = sem("d_table_stored")
        s_adj = [sem(f"adj_loaded{b}") for b in range(2)]
        s_neg = sem("negatives_checked")
        s_val = sem("candidates_found")
        s_col = sem("columns_found")
        s_find = sem("extraction_step")
        s_key = sem("key_step")
        s_hi = sem("sort_hi_step")
        s_lo = sem("sort_lo_step")
        s_stat = sem("row_stats_ready")
        s_statT = sem("row_stats_on_one_partition")
        s_cnt = sem("longest_ready")
        s_idx = sem("list_columns_ready")
        s_lst = sem("list_values_ready")
        s_iss = sem("gathers_issued")
        s_gat = [[sem(f"gathered{b}_{g}") for g in range(NG)] for b in range(2)]
        s_z = sem("z_ready")
        s_gelu = sem("gelu_done")
        s_hnow = sem("h_now_copied")
        s_newT = sem("update_transposed")
        s_prod = sem("products_ready")
        s_agg = sem("agg_summed")
        s_aggc = sem("agg_copied")
        s_dn = sem("dense_counts_ready")
        s_dstep = sem("dense_list_step")
        s_dcp = sem("dense_keys_copied")
        s_dco = sem("dense_columns_copied")
        s_hadd = sem("h_added")
        s_xb = sem("x_plus_bias_ready")
        s_dlist = sem("dense_rows_listed")
        s_drow = [sem(f"dense_adj_loaded{b}") for b in range(2)]
        s_dsc = sem("dense_s_ready")
        s_dscc = sem("dense_s_copied")
        s_dg = sem("dense_gelu_done")
        s_dsum = sem("dense_sum_done")
        s_end = sem("dense_path_done")
        s_up = sem("update_ready")
        s_upg = sem("update_gelu_done")
        s_fin = sem("final_step")
        s_nrm = sem("normalized")
        s_scl = sem("scaled")
        s_y = sem("output_ready")
        s_out = sem("output_stored")

        s_held = {e: sem(f"held_{e}") for e in ("sp", "pool", "act", "pe", "dve")}

        block = ctx.enter_context(nc.Block())

        def holder(eng, held):
            def hold(semaphore, value):
                eng.wait_ge(semaphore, value)
                eng.sem_inc(held, 1)
            return hold

        parts_of = adj[0:P, :].rearrange("(n r) (c q s) -> n r q c s", r=RP, q=PARTS, s=SEG)
        rows_of = lambda n: adj[ds((n - PARTS + 1) * P, P), :]
        loaded = lambda k, parts: 16 * PARTS * (k + 1) if parts else 16 * (k - VP + 1) + 16 * PARTS * VP

        @block.sync
        def _(sp):
            hold = holder(sp, s_held["sp"])
            for q in range(Q):
                sp.dma_start(x_sb[:, q * QD:(q + 1) * QD].rearrange("p (t d) -> p t d", d=D),
                             x[4 * q * P:4 * (q + 1) * P, :].rearrange("(t p) d -> p t d", p=P)).then_inc(s_x[q], 16)
            sp.dma_start(msg_sb, msg_w).then_inc(s_w, 16)
            sp.dma_start(upd_sb, upd_w).then_inc(s_w, 16)
            for dst, src in ((msgb_row, msg_b), (lnw_row, ln_w), (lnb_row, ln_b)):
                sp.dma_start(dst[:], src.partition_broadcast(P)).then_inc(s_rows, 16)
            sp.dma_start(updb_col[:], upd_b.rearrange("(n a) -> n a", a=1)).then_inc(s_rows, 16)
            sp.dma_start(msgb_col[:], msg_b.rearrange("(n a) -> n a", a=1)).then_inc(s_rows, 16)
            with sp.Fori(0, VP) as k:
                for b in range(2):
                    sp.wait_ge(s_col, 2 * k + b + 1)
                    sp.wait_ge(s_neg, 2 * k + b + 1)
                    for q in range(PARTS):
                        sp.dma_start(adj_sb[q:P:PARTS, b, 0:PW].rearrange("r (c s) -> r c s", s=SEG),
                                     parts_of[ds(2 * k + b, 1), :, q, :, :].rearrange("n r c s -> (n r) c s"))\
                            .then_inc(s_adj[b], 16)

            def load_rows(n, b):
                sp.wait_ge(s_col, n + 1)
                sp.wait_ge(s_neg, n + 1)
                sp.dma_start(adj_sb[:, b, :], rows_of(n)).then_inc(s_adj[b], 16)

            with sp.Fori(VP, PAIRS) as k:
                load_rows(2 * k, 0)
                load_rows(2 * k + 1, 1)
            load_rows(NT - 1, 0)
            sp.wait_ge(s_dn, 1)
            rows = sp.alloc_register("sp_rows")
            sp.reg_mov(rows, 0)
            rounds = sp.alloc_register("sp_rounds")
            sp.reg_mov(rounds, 0)
            with sp.Fori(0, T) as t:
                n = sp.value_load(dense_n[0:1, ds(t, 1)], min_val=0, max_val=P)
                with sp.If(n > 0):
                    with sp.Fori(0, P // 8) as r:
                        with sp.If(n > r * 8):
                            hold(s_dlist, sp.snap(rounds, min_val=0, max_val=N // 8) + 1)
                            for j in range(8):
                                with sp.If(n > r * 8 + j):
                                    i = sp.value_load(row8_i[0:1, j:j + 1], min_val=0, max_val=P - 1)
                                    sp.wait_ge(s_dsum, sp.snap(rows, min_val=0, max_val=N) + (2 if j == 0 else 1))
                                    sp.dma_start(adj_sb[:, j % 2, :],
                                                 adj[ds(t * P + i, 1), :].partition_broadcast(P))\
                                        .then_inc(s_drow[j % 2], 16)
                                    sp.reg_add(rows, rows, 1)
                            sp.reg_add(rounds, rounds, 1)
            with sp.Fori(0, Q) as q:
                sp.wait_ge(s_y, q + 1)
                sp.dma_start(out.rearrange("(t p) d -> p t d", p=P)[:, ds(4 * q, 4), :],
                             f_sb.rearrange("p (t d) -> p t d", d=D)[:, ds(4 * q, 4), :])\
                    .then_inc(s_out, 16)
            sp.wait_ge(s_out, 16 * Q)

        @block.gpsimd
        def _(pool):
            hold = holder(pool, s_held["pool"])
            pool.sem_inc(s_iss, 2)
            pool.memset(ident[:], 0.0).then_inc(s_const, 1)
            pool.memset(same_row[:], 1.0).then_inc(s_const, 1)
            pool.iota(iota_c, pattern=[[1, SEG], [0, 8]], base=0, channel_multiplier=0).then_inc(s_const, 1)
            pool.wait_ge(s_const, 3)
            pool.affine_select(out=ident[:], in_=ident[:], compare_op=ALU.not_equal, fill=1.0,
                               base=0, pattern=[[-1, P]], channel_multiplier=1).then_inc(s_const, 1)
            pool.iota(iota_p, pattern=[[0, CAND]], base=0, channel_multiplier=1).then_inc(s_const, 1)
            pool.iota(number_i[:], pattern=[[1, P]], base=1, channel_multiplier=0).then_inc(s_const, 1)
            block = same_row[:].rearrange("p (a b) -> p a b", b=PARTS)
            pool.affine_select(out=block, in_=block, compare_op=ALU.is_ge, fill=0.0, base=0,
                               pattern=[[-PARTS, RP], [0, PARTS]], channel_multiplier=1).then_inc(s_const, 1)
            pool.wait_ge(s_const, 7)
            pool.affine_select(out=block, in_=block, compare_op=ALU.is_ge, fill=0.0, base=PARTS - 1,
                               pattern=[[PARTS, RP], [0, PARTS]], channel_multiplier=-1).then_inc(s_const, 1)
            with pool.Fori(0, Q) as q:
                pool.wait_ge(s_drc, q + 1)
                pool.dma_start(table.ap().rearrange("(t p) d -> p t d", p=P)[:, ds(4 * q, 4), :],
                               d_rows.rearrange("p (t d) -> p t d", d=D)[:, ds(4 * q, 4), :])\
                    .then_inc(s_tab, 16)
            pool.wait_ge(s_tab, 16 * Q)

            def gathers(t, b):
                pool.wait_ge(s_idx, t + 1)
                hold(s_agg, t + 1)
                n = pool.value_load(longest[0:1, b:b + 1], min_val=0, max_val=SLOTS)
                for g0 in range(0, NG, 4):
                    with pool.If(n > G * g0):
                        for g in range(g0, g0 + 4):
                            with pool.If(n > G * g):
                                for s in range(G * g, G * g + G):
                                    pool.indirect_dma_start(
                                        out=slot[:, b, s, :], out_offset=None, in_=table.ap(),
                                        in_offset=bass.IndirectOffsetOnAxis(ap=idx[:, b, s:s + 1], axis=0))\
                                        .then_inc(s_gat[b][g], 16)
                        pool.nop()
                pool.sem_inc(s_iss, 1)

            with pool.Fori(0, PAIRS) as k:
                gathers(2 * k, 0)
                gathers(2 * k + 1, 1)
            gathers(NT - 1, 0)

        @block.scalar
        def _(act):
            hold = holder(act, s_held["act"])
            act.sem_inc(s_neg, 2)
            act.sem_inc(s_gelu, 2)
            act.sem_inc(s_aggc, 2)
            act.wait_ge(s_ln, 2)
            act.activation(std[:], mean_var[:, :, 1], ACT.Sqrt).then_inc(s_std, 1)
            act.preload_act_table_set("gelu_and_others")
            act.wait_ge(s_ln, 4)
            with act.Fori(0, Q) as q:
                for j in range(4):
                    at = ds((4 * q + j) * D, D)
                    last = act.activation(h[:, at], x_sb[:, at], ACT.Relu,
                                          bias=shift[:, ds(4 * q + j, 1)], scale=rstd[:, ds(4 * q + j, 1)])
                last.then_inc(s_h, 1)
            act.wait_ge(s_rows, 80)
            with act.Fori(0, Q) as q:
                act.wait_ge(s_dT, q + 1)
                act.activation(dT[:, ds(q * QD, QD)], work_ps[1][:], ACT.Identity,
                               bias=msgb_col[:, 0:1]).then_inc(s_dTc, 1)

            def negatives(u, k, b, parts=False):
                act.wait_ge(s_adj[b], loaded(k, parts))
                if not isinstance(u, int):
                    act.wait_ge(s_stat, u - 1)
                act.wait_ge(s_neg, u + 2)
                w = PW if parts else N
                act.activation(below[:, 0:w], adj_sb[:, b, 0:w], ACT.Relu, scale=-1.0,
                               accum_out=neg[:, b:b + 1]).then_inc(s_neg, 1)

            def copy_h(u, b, parts=False):
                if parts:
                    act.activation(h_now[:, b, :].rearrange("p (r q) -> p r q", q=PARTS),
                                   hT[:, ds(u * RP, RP)].unsqueeze(2).to_broadcast([P, RP, PARTS]),
                                   ACT.Copy).then_inc(s_hnow, 1)
                else:
                    act.activation(h_now[:, b, :], hT[:, ds((u - PARTS + 1) * P, P)], ACT.Copy).then_inc(s_hnow, 1)

            def gelus(t, b, parts=False):
                hold(s_cnt, t + 1)
                n = act.value_load(longest[0:1, b:b + 1], min_val=0, max_val=SLOTS)
                for g0 in range(0, NG, 4):
                    with act.If(n > G * g0):
                        for g in range(g0, g0 + 4):
                            with act.If(n > G * g):
                                act.wait_ge(s_z, t * NG + g + 1)
                                act.activation(slot[:, b, G * g:G * g + G, :].rearrange("p s d -> p (s d)"),
                                               z_ps[g % 2][:], ACT.Gelu).then_inc(s_gelu, 1)
                            with act.Else():
                                act.wait_ge(s_gelu, t * NG + g + 2)
                                act.sem_inc(s_gelu, 1)
                        act.nop()
                    with act.Else():
                        act.wait_ge(s_gelu, t * NG + g0 + 2)
                        act.sem_inc(s_gelu, 4)
                act.wait_ge(s_agg, t + 3)
                to = agg_parts[:, ds(t * P, P)] if parts else aggT[:, ds((t - PARTS + 1) * P, P)]
                act.activation(to, agg_ps[b][:, 0:P], ACT.Copy).then_inc(s_aggc, 1)

            negatives(0, 0, 0, True)
            negatives(1, 0, 1, True)
            copy_h(0, 0, True)
            with act.Fori(0, VP - 1) as k:
                for b in range(2):
                    negatives(2 * k + b + 2, k + 1, b, True)
                    copy_h(2 * k + b + 1, 1 - b, True)
                    gelus(2 * k + b, b, True)
            with act.Fori(VP - 1, VP) as k:
                negatives(2 * k + 2, k + 1, 0)
                copy_h(2 * k + 1, 1, True)
                gelus(2 * k, 0, True)
                negatives(2 * k + 3, k + 1, 1)
                copy_h(2 * k + 2, 0)
                gelus(2 * k + 1, 1, True)
            with act.Fori(VP, PAIRS - 1) as k:
                for b in range(2):
                    negatives(2 * k + b + 2, k + 1, b)
                    copy_h(2 * k + b + 1, 1 - b)
                    gelus(2 * k + b, b)
            act.wait_ge(s_stat, NT - 2)
            negatives(NT - 1, PAIRS, 0)
            copy_h(NT - 2, 1)
            gelus(NT - 3, 0)
            copy_h(NT - 1, 0)
            gelus(NT - 2, 1)
            gelus(NT - 1, 0)

            act.wait_ge(s_dn, 1)
            act.sem_inc(s_dscc, 2)
            rows = act.alloc_register("act_rows")
            act.reg_mov(rows, 0)
            with act.Fori(0, T) as t:
                n = act.value_load(dense_n[0:1, ds(t, 1)], min_val=0, max_val=P)
                with act.If(n > 0):
                    with act.Fori(0, P // 8) as r:
                        with act.If(n > r * 8):
                            for j in range(8):
                                with act.If(n > r * 8 + j):
                                    c = act.snap(rows, min_val=0, max_val=N)
                                    act.wait_ge(s_dsc, c + 1)
                                    act.wait_ge(s_dsum, c + (2 if j == 0 else 1))
                                    act.activation(s_colm[:, j % 2:j % 2 + 1], work_ps[j % 2][:, 0:1],
                                                   ACT.Copy).then_inc(s_dscc, 1)
                                    act.wait_ge(s_dscc, c + 3)
                                    act.activation(g_row[j % 2], dT[:], ACT.Gelu,
                                                   bias=s_colm[:, j % 2:j % 2 + 1]).then_inc(s_dg, 1)
                                    act.reg_add(rows, rows, 1)
            with act.Fori(0, Q) as q:
                act.wait_ge(s_up, q + 1)
                act.wait_ge(s_hadd, q + 1)
                act.activation(new_T, work_ps[0][:], ACT.Gelu, bias=updb_col[:, 0:1]).then_inc(s_upg, 1)
            act.wait_ge(s_fin, 2)
            act.activation(std[:], mean_var[:, :, 1], ACT.Sqrt).then_inc(s_std, 1)
            act.wait_ge(s_fin, 4)
            with act.Fori(0, Q) as q:
                for j in range(4):
                    at = ds((4 * q + j) * D, D)
                    last = act.activation(f_sb[:, at], f_sb[:, at], ACT.Identity,
                                          bias=shift[:, ds(4 * q + j, 1)], scale=rstd[:, ds(4 * q + j, 1)])
                last.then_inc(s_nrm, 1)

        @block.tensor
        def _(pe):
            hold = holder(pe, s_held["pe"])
            pe.sem_inc(s_agg, 2)
            pe.wait_ge(s_w, 32)
            pe.wait_ge(s_const, 8)
            for j, (w, half) in enumerate(((msg_sb, 0), (msg_sb, 1), (upd_sb, 0), (upd_sb, 1))):
                last = pe.transpose(z_ps[0][:, j * D:(j + 1) * D], w[:, half * D:(half + 1) * D], ident[:])
            last.then_inc(s_wT, 1)
            pe.wait_ge(s_wTc, 1)
            for q in range(Q):
                pe.wait_ge(s_h, q + 1)
                for j in range(4):
                    last = pe.transpose(z_ps[1][:, j * P:(j + 1) * P], h[:, (4 * q + j) * D:(4 * q + j + 1) * D],
                                        ident[:])
                last.then_inc(s_hTp, 1)
                pe.wait_ge(s_hT, q + 1)
                if q:
                    pe.wait_ge(s_drc, q)
                for j in range(4):
                    last = pe.matmul(work_ps[0][:, j * D:(j + 1) * D], hT[:, (4 * q + j) * P:(4 * q + j + 1) * P], w_dT[:],
                                     start=True, stop=True)
                last.then_inc(s_dr, 1)
                if q:
                    pe.wait_ge(s_dTc, q)
                pe.matmul(work_ps[1][:], w_dT[:], hT[:, q * QD:(q + 1) * QD], start=True, stop=True).then_inc(s_dT, 1)

            def stats(u, parts=False):
                pe.wait_ge(s_stat, u + 1)
                pe.wait_ge(s_cnt, u)
                pe.matmul(stat_ps[0:1, 0:P], row_stat[:, 0:1], ident[:], start=True, stop=True)
                pe.matmul(stat_ps[0:1, P:2 * P], row_stat[:, 1:2], ident[:], start=True, stop=True)
                pe.matmul(or_ps, (same_row if parts else ident)[:], row_stat[:, 1:2], start=True, stop=True)\
                    .then_inc(s_statT, 1)

            w_s4 = w_sT[:].unsqueeze(1).to_broadcast([P, G, D])

            def tile_sums(t, b):
                hold(s_cnt, t + 1)
                n = pe.value_load(longest[0:1, b:b + 1], min_val=0, max_val=SLOTS)
                pe.wait_ge(s_aggc, t + 1)
                pe.matmul(agg_ps[b][:, 0:P], zeros[:], zeros[:], start=True, stop=False)
                pe.wait_ge(s_hnow, t + 1)

                def z_of(g):
                    pe.wait_ge(s_gat[b][g], pe.snap(due[b][g], min_val=16 * G, max_val=16 * G * PAIRS))
                    pe.reg_add(due[b][g], due[b][g], 16 * G)
                    pe.wait_ge(s_gelu, t * NG + g + 1)
                    pe.matmul(z_ps[g % 2][:], ident[:],
                              slot[:, b, G * g:G * g + G, :].rearrange("p s d -> p (s d)"), start=True, stop=False)
                    pe.matmul(z_ps[g % 2][:].rearrange("p (s d) -> p s d", s=G), h_now[:, b, :], w_s4,
                              start=False, stop=True).then_inc(s_z, 1)

                def sum_of(g):
                    pe.wait_ge(s_prod, t * NG + g + 1)
                    for s in range(G * g, G * g + G):
                        pe.matmul(agg_ps[b][:, 0:P], slot[:, b, s, :], ident[:], start=False, stop=False)

                for g0 in range(0, NG, 4):
                    with pe.If(n > G * g0):
                        for g in range(g0, g0 + 4):
                            with pe.If(n > G * g):
                                z_of(g)
                            with pe.Else():
                                pe.wait_ge(s_z, t * NG + g)
                                pe.sem_inc(s_z, 1)
                        pe.nop()
                    with pe.Else():
                        pe.wait_ge(s_z, t * NG + g0)
                        pe.sem_inc(s_z, 4)
                for g0 in range(0, NG, 4):
                    with pe.If(n > G * g0):
                        for g in range(g0, g0 + 4):
                            with pe.If(n > G * g):
                                sum_of(g)
                        pe.nop()
                pe.matmul(agg_ps[b][:, 0:P], zeros[:], zeros[:], start=False, stop=True).then_inc(s_agg, 1)

            due = [[pe.alloc_register(f"due{b}_{g}") for g in range(NG)] for b in range(2)]
            for b in range(2):
                for g in range(NG):
                    pe.reg_mov(due[b][g], 16 * G)
            stats(0, True)
            stats(1, True)
            with pe.Fori(0, VP - 1) as k:
                for b in range(2):
                    tile_sums(2 * k + b, b)
                    stats(2 * k + b + 2, True)
            with pe.Fori(VP - 1, PAIRS - 1) as k:
                for b in range(2):
                    tile_sums(2 * k + b, b)
                    stats(2 * k + b + 2)
            tile_sums(NT - 3, 0)
            stats(NT - 1)
            tile_sums(NT - 2, 1)
            tile_sums(NT - 1, 0)

            pe.wait_ge(s_dn, 1)
            rows = pe.alloc_register("pe_rows")
            pe.reg_mov(rows, 0)
            rounds = pe.alloc_register("pe_rounds")
            pe.reg_mov(rounds, 0)
            with pe.Fori(0, T) as t:
                n = pe.value_load(dense_n[0:1, ds(t, 1)], min_val=0, max_val=P)
                with pe.If(n > 0):
                    with pe.Fori(0, P // 8) as r:
                        with pe.If(n > r * 8):
                            hold(s_dlist, pe.snap(rounds, min_val=0, max_val=N // 8) + 1)
                            for j in range(8):
                                with pe.If(n > r * 8 + j):
                                    i = pe.value_load(row8_i[0:1, j:j + 1], min_val=0, max_val=P - 1)
                                    pe.wait_ge(s_dscc, pe.snap(rows, min_val=0, max_val=N) + (2 if j == 0 else 1))
                                    pe.matmul(work_ps[j % 2][:, 0:1], w_sT[:], hT[:, ds(t * P + i, 1)],
                                              start=True, stop=True).then_inc(s_dsc, 1)
                                    pe.reg_add(rows, rows, 1)
                            pe.reg_add(rounds, rounds, 1)

            pe.wait_ge(s_end, 1)
            with pe.Fori(0, Q) as q:
                pe.matmul(work_ps[0][:], w_hT[:], hT[:, ds(q * QD, QD)], start=True, stop=False)
                pe.matmul(work_ps[0][:], w_aT[:], aggT[:, ds(q * QD, QD)], start=False, stop=True).then_inc(s_up, 1)
                pe.wait_ge(s_upg, q + 1)
                pe.wait_ge(s_hadd, q + 1)
                for j in range(4):
                    last = pe.transpose(work_ps[1][:, j * P:(j + 1) * P], new_T[:, j * P:(j + 1) * P], ident[:])
                last.then_inc(s_newT, 1)

        @block.vector
        def _(dve):
            hold = holder(dve, s_held["dve"])
            dve.sem_inc(s_col, 2)
            dve.sem_inc(s_dco, 1)
            dve.sem_inc(s_dsum, 2)
            dve.memset(zeros[:], 0.0)
            dve.memset(sort_hi[:], 0)
            dve.memset(sort_lo[:], 0)
            dve.wait_ge(s_const, 8)
            dve.tensor_scalar(seg_code[:], iota_c, 16, VALID, ALU.logical_shift_left, ALU.bitwise_or)
            dve.tensor_copy(number[:], number_i[:])
            dve.tensor_scalar(iota_p, iota_p, PARTS - 1, 20, ALU.bitwise_and, ALU.logical_shift_left)\
                .then_inc(s_cdve, 1)
            dve.wait_ge(s_cdve, 1)
            dve.tensor_tensor(part_code[:], seg_code[:], iota_p, ALU.bitwise_or).then_inc(s_cdve, 1)

            def norm_stats(src, s_in, first, step, arrived=None):
                for t in range(T):
                    if arrived and t % 4 == 0:
                        dve.wait_ge(arrived[t // 4], 16)
                    last = dve.bn_stats(stats6[:, t, :], src[:, t * D:(t + 1) * D])
                last.then_inc(step, 1)
                dve.wait_ge(step, 1)
                for t in range(T):
                    last = dve.bn_aggr(mean_var[:, t, :], stats6[:, t, :])
                last.then_inc(s_cdve, 1)
                dve.wait_ge(s_cdve, first)
                dve.tensor_scalar(mean_var[:, :, 1], mean_var[:, :, 1], EPS, None, ALU.add).then_inc(step, 1)
                dve.wait_ge(s_std, s_in)
                dve.reciprocal(rstd[:], std[:]).then_inc(step, 1)
                dve.wait_ge(step, 3)
                dve.scalar_tensor_tensor(shift[:], mean_var[:, :, 0], -1.0, rstd[:], ALU.mult, ALU.mult)\
                    .then_inc(step, 1)

            norm_stats(x_sb, 1, 3, s_ln, s_x)
            dve.wait_ge(s_wT, 1)
            for j, w in enumerate((w_sT, w_dT, w_hT, w_aT)):
                last = dve.tensor_copy(w[:], z_ps[0][:, j * D:(j + 1) * D])
            last.then_inc(s_wTc, 1)
            dve.wait_ge(s_rows, 80)
            with dve.Fori(0, Q) as q:
                dve.wait_ge(s_hTp, q + 1)
                dve.tensor_copy(hT[:, ds(q * QD, QD)], z_ps[1][:]).then_inc(s_hT, 1)
                dve.wait_ge(s_dr, q + 1)
                dve.tensor_tensor(d_rows[:, ds(q * QD, QD)].rearrange("p (t d) -> p t d", d=D),
                                  work_ps[0][:].rearrange("p (t d) -> p t d", d=D),
                                  msgb_row[:].unsqueeze(1).to_broadcast([P, 4, D]), ALU.add).then_inc(s_drc, 1)

            def find(u, k, b, parts=False):
                done = lambda n: dve.wait_ge(s_find, 3 * u + n)
                hold(s_adj[b], loaded(k, parts))
                seg = adj_sb[:, b, 0:PW if parts else N].rearrange("p (c s) -> p s c", s=SEG)
                for s in range(SEG):
                    last = dve.max(vals[:, b, 8 * s:8 * s + 8], seg[:, s, :])
                last.then_inc(s_val, 1)
                hold(s_val, u + 1)
                for s in range(SEG):
                    last = dve.max_index(cols[:, 8 * s:8 * s + 8], vals[:, b, 8 * s:8 * s + 8], seg[:, s, :])
                last.then_inc(s_col, 1)
                dve.tensor_reduce(seg_full[:], vals[:, b, :].rearrange("p (s e) -> p s e", e=8)[:, :, 7], AX_X, ALU.max)
                dve.tensor_scalar(used[:], vals[:, b, :], 0.0, None, ALU.not_equal, ALU.add, accum_out=n_used[:])\
                    .then_inc(s_find, 1)
                dve.wait_ge(s_col, u + 3)
                dve.scalar_tensor_tensor(code[:, b, :], cols[:], 23 if parts else 20,
                                         (part_code if parts else seg_code)[:].bitcast(u32),
                                         ALU.logical_shift_left, ALU.bitwise_or)
                done(1)
                dve.wait_ge(s_neg, u + 3)
                dve.scalar_tensor_tensor(why1[:], seg_full[:], 0.0, neg[:, b:b + 1], ALU.not_equal, ALU.add)\
                    .then_inc(s_find, 1)
                done(2)
                dve.scalar_tensor_tensor(why2[:], n_used[:], float(SLOTS), why1[:], ALU.is_gt, ALU.add)\
                    .then_inc(s_find, 1)
                done(3)
                if not (isinstance(u, int) and u == 0):
                    dve.wait_ge(s_statT, u)
                dve.scalar_tensor_tensor(row_stat[:, 0:1], why2[:], 0.0, n_used[:], ALU.is_equal, ALU.mult)
                dve.tensor_scalar(row_stat[:, 1:2], why2[:], 0.0, None, ALU.not_equal).then_inc(s_stat, 1)

            def sort(u, b):
                done = lambda n: dve.wait_ge(s_key, 4 * u + n)
                dve.wait_ge(s_statT, u + 1)
                dve.wait_ge(s_iss, u + 1)
                dve.wait_ge(s_aggc, u + 1)
                dve.tensor_scalar(row_ok[:], or_ps, 0.0, None, ALU.is_equal).then_inc(s_key, 1)
                dve.tensor_reduce(longest[0:1, b:b + 1], stat_ps[0:1, 0:P], AX_X, ALU.max)
                dve.tensor_copy(dense_flag[0:1, ds(u * P, P)], stat_ps[0:1, P:2 * P]).then_inc(s_cnt, 1)
                done(1)
                dve.tensor_scalar(kept[:], vals[:, b, :], row_ok[:, 0:1], None, ALU.mult).then_inc(s_key, 1)
                done(2)
                dve.scalar_tensor_tensor(code_kept[:].bitcast(fp32), kept[:], 0.0, code[:, b, :].bitcast(fp32),
                                         ALU.not_equal, ALU.mult).then_inc(s_key, 1)
                done(3)
                dve.scalar_tensor_tensor(key_hi[:], kept[:].bitcast(u32), 16, code_kept[:],
                                         ALU.logical_shift_right, ALU.bitwise_or).then_inc(s_hi, 1)
                dve.scalar_tensor_tensor(key_lo[:], kept[:].bitcast(u32), HALF, code_kept[:],
                                         ALU.bitwise_and, ALU.bitwise_or).then_inc(s_lo, 1)
                hold(s_cnt, u + 1)
                n = dve.value_load(longest[0:1, b:b + 1], min_val=0, max_val=SLOTS)
                f_hi, f_lo = key_hi[:].bitcast(fp32), key_lo[:].bitcast(fp32)
                t_hi, t_lo = sort_hi[:].bitcast(fp32), sort_lo[:].bitcast(fp32)
                per = 2 * RANKS + 1

                def rank(r):
                    at = slice(8 * r, 8 * r + 8)
                    hold(s_hi, per * u + 2 * r + 1)
                    dve.max(t_hi[:, at], f_hi).then_inc(s_hi, 1)
                    hold(s_lo, per * u + 2 * r + 1)
                    dve.max(t_lo[:, at], f_lo).then_inc(s_lo, 1)
                    hold(s_hi, per * u + 2 * r + 2)
                    dve.match_replace(f_hi, t_hi[:, at], f_hi, 0.0).then_inc(s_hi, 1)
                    hold(s_lo, per * u + 2 * r + 2)
                    dve.match_replace(f_lo, t_lo[:, at], f_lo, 0.0).then_inc(s_lo, 1)

                for r in range(SURE):
                    rank(r)
                with dve.If(n > 8 * SURE):
                    rank(SURE)
                    for r in range(SURE + 1, RANKS):
                        with dve.If(n > 8 * r):
                            rank(r)
                        with dve.Else():
                            dve.wait_ge(s_hi, per * u + 2 * r + 1)
                            dve.sem_inc(s_hi, 2)
                            dve.wait_ge(s_lo, per * u + 2 * r + 1)
                            dve.sem_inc(s_lo, 2)
                    dve.nop()
                with dve.Else():
                    dve.wait_ge(s_hi, per * u + 2 * SURE + 1)
                    dve.sem_inc(s_hi, 2 * (RANKS - SURE))
                    dve.wait_ge(s_lo, per * u + 2 * SURE + 1)
                    dve.sem_inc(s_lo, 2 * (RANKS - SURE))
                dve.wait_ge(s_hi, per * u + per)
                dve.tensor_scalar(idx[:, b, :].bitcast(u32), sort_hi[:], 16, 0xFFF,
                                  ALU.logical_shift_right, ALU.bitwise_and).then_inc(s_idx, 1)
                dve.tensor_scalar(val_hi[:], sort_hi[:], HALF, 16, ALU.bitwise_and, ALU.logical_shift_left)\
                    .then_inc(s_key, 1)
                done(4)
                dve.wait_ge(s_lo, per * u + per)
                dve.scalar_tensor_tensor(val[:, b, :], sort_lo[:], HALF, val_hi[:],
                                         ALU.bitwise_and, ALU.bitwise_or).then_inc(s_lst, 1)

            def products(t, b):
                n = dve.value_load(longest[0:1, b:b + 1], min_val=0, max_val=SLOTS)
                hold(s_lst, t + 1)
                for g0 in range(0, NG, 4):
                    with dve.If(n > G * g0):
                        for g in range(g0, g0 + 4):
                            with dve.If(n > G * g):
                                dve.wait_ge(s_gelu, t * NG + g + 3)
                                at = slot[:, b, G * g:G * g + G, :]
                                v = val[:, b, G * g:G * g + G].bitcast(fp32)
                                dve.tensor_tensor(at, at, v.unsqueeze(2).to_broadcast([P, G, D]), ALU.mult)\
                                    .then_inc(s_prod, 1)
                            with dve.Else():
                                dve.wait_ge(s_prod, t * NG + g)
                                dve.sem_inc(s_prod, 1)
                        dve.nop()
                    with dve.Else():
                        dve.wait_ge(s_prod, t * NG + g0)
                        dve.sem_inc(s_prod, 4)

            find(0, 0, 0, True)
            find(1, 0, 1, True)
            sort(0, 0)
            with dve.Fori(0, VP - 1) as k:
                for b in range(2):
                    find(2 * k + b + 2, k + 1, b, True)
                    sort(2 * k + b + 1, 1 - b)
                    products(2 * k + b, b)
            with dve.Fori(VP - 1, PAIRS - 1) as k:
                for b in range(2):
                    find(2 * k + b + 2, k + 1, b)
                    sort(2 * k + b + 1, 1 - b)
                    products(2 * k + b, b)
            find(NT - 1, PAIRS, 0)
            sort(NT - 2, 1)
            products(NT - 3, 0)
            sort(NT - 1, 0)
            products(NT - 2, 1)
            products(NT - 1, 0)

            dve.wait_ge(s_aggc, NT + 2)
            with nc.allow_low_precision("flags of 0 and 1, and counts up to 128"):
                dve.tensor_reduce(first_flag[:], dense_flag[0:1, 0:PARTS * P].rearrange("a (r q) -> a r q", q=PARTS),
                                  AX_X, ALU.max).then_inc(s_cdve, 1)
                dve.tensor_reduce(aggT[:, 0:P], agg_parts[:].rearrange("p (r q) -> p r q", q=PARTS), AX_X, ALU.add)
                dve.wait_ge(s_cdve, 4)
                rows_flag = dense_flag[0:1, (PARTS - 1) * P:NT * P]
                dve.tensor_copy(rows_flag[:, 0:P], first_flag[:]).then_inc(s_cdve, 1)
                dve.wait_ge(s_cdve, 5)
                dve.tensor_reduce(dense_n[:], rows_flag.rearrange("a (t p) -> a t p", p=P), AX_X, ALU.add)\
                    .then_inc(s_dn, 1)
            dve.wait_ge(s_dn, 1)
            due = [dve.alloc_register(f"dense_adj_due{b}") for b in range(2)]
            rows, rounds, tiles = (dve.alloc_register(f"dve_{x}") for x in ("rows", "rounds", "tiles"))
            for reg, value in ((due[0], 16), (due[1], 16), (rows, 0), (rounds, 0), (tiles, 1)):
                dve.reg_mov(reg, value)
            with dve.Fori(0, T) as t:
                n = dve.value_load(dense_n[0:1, ds(t, 1)], min_val=0, max_val=P)
                with dve.If(n > 0):
                    dve.tensor_tensor(tile_key[:], rows_flag[:, ds(t * P, P)], number[:], ALU.mult).then_inc(s_dcp, 1)
                    hold(s_dcp, dve.snap(tiles, min_val=1, max_val=T))
                    dve.reg_add(tiles, tiles, 1)
                    with dve.Fori(0, P // 8) as r:
                        with dve.If(n > r * 8):
                            c = dve.snap(rounds, min_val=0, max_val=N // 8)
                            dve.max(key8[:], tile_key[:]).then_inc(s_dstep, 1)
                            hold(s_dstep, c * 2 + 1)
                            dve.match_replace(tile_key[:], key8[:], tile_key[:], 0.0).then_inc(s_dstep, 1)
                            dve.tensor_scalar(row8_i[:], key8[:], -1.0, 0.0, ALU.add, ALU.max).then_inc(s_dlist, 1)
                            hold(s_dlist, c + 1)
                            for j in range(8):
                                with dve.If(n > r * 8 + j):
                                    i = dve.value_load(row8_i[0:1, j:j + 1], min_val=0, max_val=P - 1)
                                    d = dve.snap(rows, min_val=0, max_val=N)
                                    arrived = dve.snap(due[j % 2], min_val=16, max_val=16 * N)
                                    dve.wait_ge(s_dg, d + 1)
                                    dve.wait_ge(s_drow[j % 2], arrived)
                                    dve.tensor_tensor_reduce(out=g_row[j % 2], in0=g_row[j % 2],
                                                             in1=adj_sb[:, j % 2, :], scale=1.0, scalar=0.0,
                                                             op0=ALU.mult, op1=ALU.add,
                                                             accum_out=dense_sum[:, j:j + 1]).then_inc(s_dsum, 1)
                                    dve.wait_ge(s_dsum, d + 3)
                                    dve.tensor_copy(aggT[:, ds(t * P + i, 1)], dense_sum[:, j:j + 1])\
                                        .then_inc(s_dco, 1)
                                    dve.reg_add(rows, rows, 1)
                                    dve.reg_add(due[j % 2], due[j % 2], 16)
                            dve.wait_ge(s_dco, dve.snap(rows, min_val=0, max_val=N) + 1)
                            hold(s_dstep, c * 2 + 2)
                            dve.reg_add(rounds, rounds, 1)
            dve.sem_inc(s_hadd, 1)
            dve.sem_inc(s_end, 1)

            row4 = lambda r: r[:].unsqueeze(1).to_broadcast([P, 4, D])
            quad = lambda a, q: a[:, ds(q * QD, QD)].rearrange("p (t d) -> p t d", d=D)
            with dve.Fori(0, Q) as q:
                dve.wait_ge(s_newT, q + 1)
                dve.tensor_tensor(f_sb[:, ds(q * QD, QD)], work_ps[1][:], h[:, ds(q * QD, QD)],
                                  ALU.add).then_inc(s_hadd, 1)
            with dve.Fori(0, Q) as q:
                dve.tensor_tensor(quad(x_sb, q), quad(x_sb, q), row4(lnb_row), ALU.add).then_inc(s_xb, 1)
            dve.wait_ge(s_hadd, Q + 1)
            norm_stats(f_sb, 2, 6, s_fin)
            dve.wait_ge(s_xb, Q)
            with dve.Fori(0, Q) as q:
                dve.wait_ge(s_nrm, q + 1)
                dve.tensor_tensor(quad(f_sb, q), quad(f_sb, q), row4(lnw_row), ALU.mult).then_inc(s_scl, 1)
                dve.wait_ge(s_scl, q + 1)
                dve.tensor_tensor(quad(f_sb, q), quad(f_sb, q), quad(x_sb, q), ALU.add).then_inc(s_y, 1)


_INS = ["x", "adj", "L0_gnn_msg_w", "L0_gnn_msg_b", "L0_gnn_upd_w", "L0_gnn_upd_b", "L0_gnn_ln_w", "L0_gnn_ln_b"]


def kernel(**inputs):
    import numpy as _np
    import concourse.bacc as _bacc
    from concourse import mybir as _mybir
    from concourse.bass_utils import run_bass_kernel_spmd as _run

    nc = _bacc.Bacc("TRN2", target_bir_lowering=False, num_devices=1)
    arrays, args = {}, []
    for name in _INS:
        a = _np.ascontiguousarray(inputs[name])
        arrays[f"in_{name}"] = a
        args.append(nc.dram_tensor(f"in_{name}", a.shape, _mybir.dt.from_np(a.dtype), kind="ExternalInput").ap())
    shape = arrays["in_x"].shape
    args.append(nc.dram_tensor("out_0", shape, _mybir.dt.float32, kind="ExternalOutput").ap())
    gnn_sparse_rows_kernel(nc, *args)
    r = _run(nc, [arrays], core_ids=[0])
    return r.results[0]["out_0"]
```

```python
import concourse.bass as bass
from concourse import mybir
from contextlib import ExitStack


def gnn_sparse_rows_kernel(nc, x, adj, msg_w, msg_b, upd_w, upd_b, ln_w, ln_b, out):
    fp32, u8 = mybir.dt.float32, mybir.dt.uint8
    u32, i32 = mybir.dt.uint32, mybir.dt.int32
    ALU = mybir.AluOpType
    ACT = mybir.ActivationFunctionType
    AX_X = mybir.AxisListType.X
    ds = bass.ds

    N, D = x.shape
    P = 128
    assert D == P and N % (4 * P) == 0 and N <= 4096
    T = N // P
    PARTS = 8
    RP = P // PARTS
    NT = PARTS + T - 1
    assert NT % 2 == 1 and T >= 8
    PW = N // PARTS
    VP = PARTS // 2
    PAIRS = NT // 2
    Q = T // 4
    QD = 4 * D
    SEG = 16
    CAND = 8 * SEG
    SLOTS = 64
    G = 4
    NG = SLOTS // G
    RANKS = SLOTS // 8
    EPS = 1e-5
    VALID = 0x20000000
    HALF = 0xFFFF
    SURE = 3

    table = nc.dram_tensor("d_table", (N, D), fp32)
    numbers = nc.dram_tensor("row_numbers", (1, N), fp32)

    ctx = ExitStack()
    with ctx:
        def sb(name, shape, dt=fp32):
            return ctx.enter_context(nc.sbuf_tensor(name, shape, dt))

        def bank(name):
            return ctx.enter_context(nc.psum_tensor(name, [P, 512], fp32))

        def sem(name):
            return ctx.enter_context(nc.semaphore(name))

        w_sT = sb("w_sT", [P, D])
        w_dT = sb("w_dT", [P, D])
        w_hT = sb("w_hT", [P, D])
        w_aT = sb("w_aT", [P, D])
        msgb_col = sb("msgb_col", [P, 1])
        msgb_row = sb("msgb_row", [P, D])
        updb_col = sb("updb_col", [P, 1])
        lnw_row = sb("lnw_row", [P, D])
        lnb_row = sb("lnb_row", [P, D])
        ident = sb("ident", [P, P])
        same_row = sb("same_row", [P, P])
        zeros = sb("zeros", [1, P])
        seg_code = sb("seg_code", [P, CAND], i32)
        part_code = sb("part_code", [P, CAND], i32)
        h = sb("h", [P, N])
        hT = sb("hT", [P, N + P])
        dT = sb("dT", [P, N])
        x_sb = sb("x_sb", [P, N])
        agg_parts = sb("agg_parts", [P, PARTS * P])
        aggT = sb("aggT", [P, N])
        stats6 = sb("stats6", [P, T, 6])
        mean_var = sb("mean_var", [P, T, 2])
        std = sb("std", [P, T])
        rstd = sb("rstd", [P, T])
        shift = sb("shift", [P, T])
        adj_sb = sb("adj_sb", [P, 2, N])
        below = sb("below", [P, N], u8)
        neg = sb("neg", [P, 2])
        vals = sb("vals", [P, 2, CAND])
        cols = sb("cols", [P, CAND], u32)
        used = sb("used", [P, CAND])
        seg_full = sb("seg_full", [P, 1])
        n_used = sb("n_used", [P, 1])
        why1 = sb("why1", [P, 1])
        why2 = sb("why2", [P, 1])
        row_stat = sb("row_stat", [P, 2])
        row_ok = sb("row_ok", [P, 1])
        kept = sb("kept", [P, CAND])
        iota_c, iota_p = kept[:].bitcast(i32), used[:].bitcast(i32)
        code = sb("code", [P, 2, CAND], u32)
        code_kept = sb("code_kept", [P, CAND], u32)
        key_hi = sb("key_hi", [P, CAND], u32)
        key_lo = sb("key_lo", [P, CAND], u32)
        sort_hi = sb("sort_hi", [P, SLOTS], u32)
        sort_lo = sb("sort_lo", [P, SLOTS], u32)
        val_hi = sb("val_hi", [P, SLOTS], u32)
        idx = sb("idx", [P, 2, SLOTS], i32)
        val = sb("val", [P, 2, SLOTS], u32)
        longest = sb("longest", [1, 2], i32)
        dense_flag = sb("dense_flag", [1, NT * P], u8)
        first_flag = sb("first_flag", [1, P], u8)
        dense_n = sb("dense_n", [1, 1], i32)
        key8 = sb("key8", [1, 8])
        row8_i = sb("row8_i", [1, 8], i32)
        dense_sum = sb("dense_sum", [P, 8])
        s_colm = sb("s_colm", [P, 2])
        h_now = sb("h_now", [P, 2, P])
        new_T = [agg_parts[:, b * QD:(b + 1) * QD] for b in range(2)]
        slot = sb("slot", [P, 2, SLOTS, D])

        msg_sb = slot[:, 0, T:T + 2, :].rearrange("p t d -> p (t d)")
        upd_sb = slot[:, 0, T + 2:T + 4, :].rearrange("p t d -> p (t d)")
        d_rows = slot[:, 1, 0:T, :].rearrange("p t d -> p (t d)")
        f_sb = slot[:, 0, 0:T, :].rearrange("p t d -> p (t d)")
        dense_key = slot[0:1, 1, T:2 * T, :].rearrange("p s d -> p (s d)")
        dense_adj = [adj_sb[:, 0, :], adj_sb[:, 1, :], slot[:, 0, T:2 * T, :].rearrange("p s d -> p (s d)")]
        g_row = [slot[:, b, :, :].rearrange("p s d -> p (s d)")[:, 0:N] for b in range(2)]

        z_ps = [bank("z0"), bank("z1")]
        agg_ps = [bank("agg0"), bank("agg1")]
        stat_ps = bank("stat_ps")
        or_ps = stat_ps[:, 2 * P:2 * P + 1]
        work_ps = [bank("work0"), bank("work1"), bank("work2")]
        d_ps = [work_ps[0], work_ps[2], agg_ps[0], agg_ps[1]]
        up_ps = [work_ps[2], agg_ps[0], agg_ps[1], stat_ps, z_ps[1], z_ps[0]]
        new_ps = [work_ps[0], work_ps[1]]
        UP = len(up_ps)

        s_w = sem("weights_loaded")
        s_rows = sem("bias_rows_loaded")
        s_x = [sem(f"x_loaded{q}") for q in range(Q)]
        s_const = sem("constants_made")
        s_cdve = sem("dve_constant_step")
        s_wT = sem("weights_transposed")
        s_wTc = sem("weights_copied")
        s_ln = sem("layernorm_step")
        s_std = sem("std_ready")
        s_h = sem("h_ready")
        s_hTp = sem("h_transposed")
        s_hT = sem("hT_copied")
        s_dr = sem("d_rows_ready")
        s_drc = sem("d_rows_copied")
        s_dT = sem("dT_ready")
        s_dTc = sem("dT_copied")
        s_tab = sem("d_table_stored")
        s_adj = [sem(f"adj_loaded{b}") for b in range(2)]
        s_neg = sem("negatives_checked")
        s_val = sem("candidates_found")
        s_col = sem("columns_found")
        s_find = sem("extraction_step")
        s_key = sem("key_step")
        s_hi = sem("sort_hi_step")
        s_lo = sem("sort_lo_step")
        s_stat = sem("row_stats_ready")
        s_statT = sem("row_stats_on_one_partition")
        s_cnt = sem("longest_ready")
        s_idx = sem("list_columns_ready")
        s_lst = sem("list_values_ready")
        s_iss = sem("gathers_issued")
        s_gat = [[sem(f"gathered{b}_{g}") for g in range(NG)] for b in range(2)]
        s_z = sem("z_ready")
        s_gelu = sem("gelu_done")
        s_hnow = sem("h_now_copied")
        s_newT = sem("update_transposed")
        s_prod = sem("products_ready")
        s_agg = sem("agg_summed")
        s_aggc = sem("agg_copied")
        s_dn = sem("dense_counts_ready")
        s_dstep = sem("dense_list_step")
        s_num = sem("row_numbers_made")
        s_nst = sem("row_numbers_stored")
        s_nld = sem("row_numbers_loaded")
        s_dco = sem("dense_columns_copied")
        s_hadd = sem("h_added")
        s_xb = sem("x_plus_bias_ready")
        s_dlist = sem("dense_rows_listed")
        s_drow = [sem(f"dense_adj_loaded{b}") for b in range(3)]
        s_dsc = sem("dense_s_ready")
        s_dscc = sem("dense_s_copied")
        s_dg = sem("dense_gelu_done")
        s_dsum = sem("dense_sum_done")
        s_end = sem("dense_path_done")
        s_up = sem("update_ready")
        s_upg = sem("update_gelu_done")
        s_fin = sem("final_step")
        s_nrm = sem("normalized")
        s_scl = sem("scaled")
        s_y = sem("output_ready")
        s_out = sem("output_stored")

        s_held = {e: sem(f"held_{e}") for e in ("sp", "pool", "act", "pe", "dve")}

        block = ctx.enter_context(nc.Block())

        def holder(eng, held):
            def hold(semaphore, value):
                eng.wait_ge(semaphore, value)
                eng.sem_inc(held, 1)
            return hold

        def groups(eng, n, body, skip=None, g=0):
            with eng.If(n > G * g):
                body(g)
                if g + 1 < NG:
                    groups(eng, n, body, skip, g + 1)
                eng.nop()
            if skip:
                with eng.Else():
                    skip(g)

        def dense_rounds(eng, n, body):
            with eng.If(n > 0):
                body(0, lambda j: n > j)
            with eng.If(n > 8):
                with eng.Fori(0, N // 512) as i0:
                    with eng.If(n > i0 * 512 + 8):
                        with eng.Fori(0, 8) as i1:
                            with eng.If(n > i0 * 512 + i1 * 64 + 8):
                                with eng.Fori(0, 8) as i2:
                                    with eng.If(n > i0 * 512 + i1 * 64 + i2 * 8 + 8):
                                        body(i0 * 64 + i1 * 8 + i2 + 1,
                                             lambda j: n > i0 * 512 + i1 * 64 + i2 * 8 + 8 + j)

        parts_of = adj[0:P, :].rearrange("(n r) (c q s) -> n r q c s", r=RP, q=PARTS, s=SEG)
        rows_of = lambda n: adj[ds((n - PARTS + 1) * P, P), :]
        loaded = lambda k, parts: 16 * PARTS * (k + 1) if parts else 16 * (k - VP + 1) + 16 * PARTS * VP

        row4 = lambda r: r[:].unsqueeze(1).to_broadcast([P, 4, D])
        quad = lambda a, q: a[:, ds(q * QD, QD)].rearrange("p (t d) -> p t d", d=D)

        @block.sync
        def _(sp):
            hold = holder(sp, s_held["sp"])
            for q in range(Q):
                sp.dma_start(x_sb[:, q * QD:(q + 1) * QD].rearrange("p (t d) -> p t d", d=D),
                             x[4 * q * P:4 * (q + 1) * P, :].rearrange("(t p) d -> p t d", p=P)).then_inc(s_x[q], 16)
            sp.dma_start(msg_sb, msg_w).then_inc(s_w, 16)
            sp.dma_start(upd_sb, upd_w).then_inc(s_w, 16)
            for dst, src in ((msgb_row, msg_b), (lnw_row, ln_w), (lnb_row, ln_b)):
                sp.dma_start(dst[:], src.partition_broadcast(P)).then_inc(s_rows, 16)
            sp.dma_start(updb_col[:], upd_b.rearrange("(n a) -> n a", a=1)).then_inc(s_rows, 16)
            sp.dma_start(msgb_col[:], msg_b.rearrange("(n a) -> n a", a=1)).then_inc(s_rows, 16)
            with sp.Fori(0, VP) as k:
                for b in range(2):
                    sp.wait_ge(s_col, 2 * k + b + 1)
                    sp.wait_ge(s_neg, 2 * k + b + 1)
                    for q in range(PARTS):
                        sp.dma_start(adj_sb[q:P:PARTS, b, 0:PW].rearrange("r (c s) -> r c s", s=SEG),
                                     parts_of[ds(2 * k + b, 1), :, q, :, :].rearrange("n r c s -> (n r) c s"))\
                            .then_inc(s_adj[b], 16)

            def load_rows(n, b):
                sp.wait_ge(s_col, n + 1)
                sp.wait_ge(s_neg, n + 1)
                sp.dma_start(adj_sb[:, b, :], rows_of(n)).then_inc(s_adj[b], 16)

            with sp.Fori(VP, PAIRS) as k:
                load_rows(2 * k, 0)
                load_rows(2 * k + 1, 1)
            load_rows(NT - 1, 0)
            sp.wait_ge(s_agg, NT + 1)
            sp.dma_start(dense_key, numbers.ap()).then_inc(s_nld, 16)
            sp.wait_ge(s_dn, 1)
            n = sp.value_load(dense_n[0:1, 0:1], min_val=0, max_val=N)

            def dense_loads(c, in_list):
                hold(s_dlist, c + 1)
                for j in range(8):
                    with sp.If(in_list(j)):
                        i = sp.value_load(row8_i[0:1, j:j + 1], min_val=0, max_val=N - 1)
                        sp.wait_ge(s_dsum, c * 8 + max(j, 2))
                        if j == 2:
                            sp.wait_ge(s_agg, NT + 2)
                        sp.dma_start(dense_adj[j % 3], adj[ds(i, 1), :].partition_broadcast(P))\
                            .then_inc(s_drow[j % 3], 16)

            dense_rounds(sp, n, dense_loads)
            with sp.Fori(0, Q) as q:
                sp.wait_ge(s_y, q + 1)
                sp.dma_start(out.rearrange("(t p) d -> p t d", p=P)[:, ds(4 * q, 4), :],
                             f_sb.rearrange("p (t d) -> p t d", d=D)[:, ds(4 * q, 4), :])\
                    .then_inc(s_out, 16)
            sp.wait_ge(s_out, 16 * Q)

        @block.gpsimd
        def _(pool):
            hold = holder(pool, s_held["pool"])
            pool.sem_inc(s_iss, 2)
            pool.memset(ident[:], 0.0).then_inc(s_const, 1)
            pool.memset(same_row[:], 1.0).then_inc(s_const, 1)
            pool.iota(iota_c, pattern=[[1, SEG], [0, 8]], base=0, channel_multiplier=0).then_inc(s_const, 1)
            pool.wait_ge(s_const, 3)
            pool.affine_select(out=ident[:], in_=ident[:], compare_op=ALU.not_equal, fill=1.0,
                               base=0, pattern=[[-1, P]], channel_multiplier=1).then_inc(s_const, 1)
            pool.iota(iota_p, pattern=[[0, CAND]], base=0, channel_multiplier=1).then_inc(s_const, 1)
            block = same_row[:].rearrange("p (a b) -> p a b", b=PARTS)
            pool.affine_select(out=block, in_=block, compare_op=ALU.is_ge, fill=0.0, base=0,
                               pattern=[[-PARTS, RP], [0, PARTS]], channel_multiplier=1).then_inc(s_const, 1)
            pool.wait_ge(s_const, 6)
            pool.affine_select(out=block, in_=block, compare_op=ALU.is_ge, fill=0.0, base=PARTS - 1,
                               pattern=[[PARTS, RP], [0, PARTS]], channel_multiplier=-1).then_inc(s_const, 1)
            pool.iota(aggT[0:1, :].bitcast(i32), pattern=[[1, N]], base=1, channel_multiplier=0).then_inc(s_num, 1)
            pool.memset(slot[:, 0, 0:T, :], 0.0).then_inc(s_const, 1)
            pool.memset(slot[:, 0, T + 4:SLOTS, :], 0.0).then_inc(s_const, 1)
            pool.memset(slot[:, 1, T:SLOTS, :], 0.0).then_inc(s_const, 1)
            pool.wait_ge(s_const, 10)
            pool.wait_ge(s_num, 2)
            pool.dma_start(numbers.ap(), aggT[0:1, :]).then_inc(s_nst, 16)
            with pool.Fori(0, Q) as q:
                pool.wait_ge(s_drc, q + 1)
                pool.dma_start(table.ap().rearrange("(t p) d -> p t d", p=P)[:, ds(4 * q, 4), :],
                               d_rows.rearrange("p (t d) -> p t d", d=D)[:, ds(4 * q, 4), :])\
                    .then_inc(s_tab, 16)
            pool.wait_ge(s_tab, 16 * Q)
            pool.wait_ge(s_nst, 16)

            def gather(b, s):
                pool.indirect_dma_start(out=slot[:, b, s, :], out_offset=None, in_=table.ap(),
                                        in_offset=bass.IndirectOffsetOnAxis(ap=idx[:, b, s:s + 1], axis=0))\
                    .then_inc(s_gat[b][s // G], 16)

            def gathers(t, b):
                pool.wait_ge(s_idx, t + 1)
                hold(s_agg, t + 1)
                n = pool.value_load(longest[0:1, b:b + 1], min_val=0, max_val=SLOTS)
                for g0 in range(0, NG, 4):
                    with pool.If(n > G * g0):
                        for g in range(g0, g0 + 4):
                            with pool.If(n > G * g):
                                gather(b, G * g)
                                for s in range(G * g + 1, G * g + G):
                                    with pool.If(n > s):
                                        gather(b, s)
                        pool.nop()
                pool.sem_inc(s_iss, 1)

            with pool.Fori(0, PAIRS) as k:
                gathers(2 * k, 0)
                gathers(2 * k + 1, 1)
            gathers(NT - 1, 0)
            pool.wait_ge(s_rows, 80)
            with pool.Fori(0, Q) as q:
                pool.tensor_tensor(quad(x_sb, q), quad(x_sb, q), row4(lnb_row), ALU.add).then_inc(s_xb, 1)

        @block.scalar
        def _(act):
            hold = holder(act, s_held["act"])
            act.sem_inc(s_neg, 2)
            act.sem_inc(s_dTc, 1)
            act.sem_inc(s_gelu, 2)
            act.sem_inc(s_aggc, 2)
            act.wait_ge(s_num, 1)
            act.activation(aggT[0:1, :], aggT[0:1, :].bitcast(i32), ACT.Copy).then_inc(s_num, 1)
            act.wait_ge(s_ln, 2)
            act.activation(std[:], mean_var[:, :, 1], ACT.Sqrt).then_inc(s_std, 1)
            act.preload_act_table_set("gelu_and_others")
            act.wait_ge(s_ln, 4)
            def negatives(u, k, b, parts=False):
                act.wait_ge(s_adj[b], loaded(k, parts))
                if not isinstance(u, int):
                    act.wait_ge(s_stat, u - 1)
                act.wait_ge(s_neg, u + 2)
                w = PW if parts else N
                act.activation(below[:, 0:w], adj_sb[:, b, 0:w], ACT.Relu, scale=-1.0,
                               accum_out=neg[:, b:b + 1]).then_inc(s_neg, 1)

            def copy_h(u, b, parts=False):
                if parts:
                    act.activation(h_now[:, b, :].rearrange("p (r q) -> p r q", q=PARTS),
                                   hT[:, ds(u * RP, RP)].unsqueeze(2).to_broadcast([P, RP, PARTS]),
                                   ACT.Copy).then_inc(s_hnow, 1)
                else:
                    act.activation(h_now[:, b, :], hT[:, ds((u - PARTS + 1) * P, P)], ACT.Copy).then_inc(s_hnow, 1)

            def gelus(t, b, parts=False):
                act.wait_ge(s_lst, t + 1)
                hold(s_cnt, t + 1)
                n = act.value_load(longest[0:1, b:b + 1], min_val=0, max_val=SLOTS)

                def gelu(g):
                    act.wait_ge(s_z, t * NG + g + 1)
                    act.activation(slot[:, b, G * g:G * g + G, :].rearrange("p s d -> p (s d)"),
                                   z_ps[g % 2][:], ACT.Gelu).then_inc(s_gelu, 1)
                    act.wait_ge(s_gelu, t * NG + g + 3)
                    for s in range(G * g, G * g + G):
                        last = act.activation(slot[:, b, s, :], slot[:, b, s, :], ACT.Copy,
                                              scale=val[:, b, s:s + 1].bitcast(fp32))
                    last.then_inc(s_prod, 1)

                def skip(g):
                    act.wait_ge(s_gelu, t * NG + g + 2)
                    act.sem_inc(s_gelu, NG - g)
                    act.wait_ge(s_prod, t * NG + g)
                    act.sem_inc(s_prod, NG - g)

                groups(act, n, gelu, skip)
                act.wait_ge(s_agg, t + 3)
                to = agg_parts[:, ds(t * P, P)] if parts else aggT[:, ds((t - PARTS + 1) * P, P)]
                act.activation(to, agg_ps[b][:, 0:P], ACT.Copy).then_inc(s_aggc, 1)

            for q in range(Q + 1):
                if q < Q:
                    for t in range(4 * q, 4 * q + 4):
                        last = act.activation(h[:, t * D:(t + 1) * D], x_sb[:, t * D:(t + 1) * D], ACT.Relu,
                                              bias=shift[:, t:t + 1], scale=rstd[:, t:t + 1])
                    last.then_inc(s_h, 1)
                if q < 2:
                    negatives(q, 0, q, True)
                if q:
                    act.wait_ge(s_hTp, q)
                    act.activation(hT[:, (q - 1) * QD:q * QD], z_ps[(q - 1) % 2][:], ACT.Copy).then_inc(s_hT, 1)
            act.wait_ge(s_hT, Q)
            act.wait_ge(s_rows, 80)
            with act.Fori(0, Q) as q:
                act.wait_ge(s_dT, q + 1)
                act.activation(dT[:, ds(q * QD, QD)], work_ps[1][:], ACT.Identity,
                               bias=msgb_col[:, 0:1]).then_inc(s_dTc, 1)
            copy_h(0, 0, True)
            with act.Fori(0, VP - 1) as k:
                for b in range(2):
                    negatives(2 * k + b + 2, k + 1, b, True)
                    copy_h(2 * k + b + 1, 1 - b, True)
                    gelus(2 * k + b, b, True)
            with act.Fori(VP - 1, VP) as k:
                negatives(2 * k + 2, k + 1, 0)
                copy_h(2 * k + 1, 1, True)
                gelus(2 * k, 0, True)
                negatives(2 * k + 3, k + 1, 1)
                copy_h(2 * k + 2, 0)
                gelus(2 * k + 1, 1, True)
            with act.Fori(VP, PAIRS - 1) as k:
                for b in range(2):
                    negatives(2 * k + b + 2, k + 1, b)
                    copy_h(2 * k + b + 1, 1 - b)
                    gelus(2 * k + b, b)
            act.wait_ge(s_stat, NT - 2)
            negatives(NT - 1, PAIRS, 0)
            copy_h(NT - 2, 1)
            gelus(NT - 3, 0)
            copy_h(NT - 1, 0)
            gelus(NT - 2, 1)
            gelus(NT - 1, 0)

            act.wait_ge(s_dn, 1)
            act.sem_inc(s_dscc, 2)
            n = act.value_load(dense_n[0:1, 0:1], min_val=0, max_val=N)

            def dense_gelus(c, in_list):
                for j in range(8):
                    with act.If(in_list(j)):
                        act.wait_ge(s_dsc, c * 8 + j + 1)
                        act.wait_ge(s_dsum, c * 8 + j + (2 if j == 0 else 1))
                        act.activation(s_colm[:, j % 2:j % 2 + 1], work_ps[j % 2][:, 0:1],
                                       ACT.Copy).then_inc(s_dscc, 1)
                        act.wait_ge(s_dscc, c * 8 + j + 3)
                        act.activation(g_row[j % 2], dT[:], ACT.Gelu,
                                       bias=s_colm[:, j % 2:j % 2 + 1]).then_inc(s_dg, 1)

            dense_rounds(act, n, dense_gelus)
            for q in range(Q):
                act.wait_ge(s_up, q + 1)
                if q >= 2:
                    act.wait_ge(s_newT, q - 1)
                act.activation(new_T[q % 2], up_ps[q % UP][:], ACT.Gelu, bias=updb_col[:, 0:1]).then_inc(s_upg, 1)
            act.wait_ge(s_fin, 2)
            act.activation(std[:], mean_var[:, :, 1], ACT.Sqrt).then_inc(s_std, 1)
            act.wait_ge(s_fin, 4)
            with act.Fori(0, Q) as q:
                for j in range(4):
                    at = ds((4 * q + j) * D, D)
                    last = act.activation(f_sb[:, at], f_sb[:, at], ACT.Identity,
                                          bias=shift[:, ds(4 * q + j, 1)], scale=rstd[:, ds(4 * q + j, 1)])
                last.then_inc(s_nrm, 1)

        @block.tensor
        def _(pe):
            hold = holder(pe, s_held["pe"])
            pe.sem_inc(s_agg, 2)
            pe.wait_ge(s_w, 32)
            pe.wait_ge(s_const, 7)
            for j, (w, half) in enumerate(((msg_sb, 0), (msg_sb, 1), (upd_sb, 0), (upd_sb, 1))):
                last = pe.transpose(z_ps[0][:, j * D:(j + 1) * D], w[:, half * D:(half + 1) * D], ident[:])
            last.then_inc(s_wT, 1)
            pe.wait_ge(s_wTc, 1)
            def stats(u, parts=False):
                pe.wait_ge(s_stat, u + 1)
                pe.wait_ge(s_cnt, u)
                pe.matmul(stat_ps[0:1, 0:P], row_stat[:, 0:1], ident[:], start=True, stop=True)
                pe.matmul(stat_ps[0:1, P:2 * P], row_stat[:, 1:2], ident[:], start=True, stop=True)
                pe.matmul(or_ps, (same_row if parts else ident)[:], row_stat[:, 1:2], start=True, stop=True)\
                    .then_inc(s_statT, 1)

            w_s4 = w_sT[:].unsqueeze(1).to_broadcast([P, G, D])

            def tile_sums(t, b):
                hold(s_cnt, t + 1)
                n = pe.value_load(longest[0:1, b:b + 1], min_val=0, max_val=SLOTS)
                pe.wait_ge(s_aggc, t + 1)
                pe.matmul(agg_ps[b][:, 0:P], zeros[:], zeros[:], start=True, stop=False)
                pe.wait_ge(s_hnow, t + 1)

                def z_of(g):
                    with pe.If(n > G * g + G - 1):
                        pe.reg_add(due[b][g], due[b][g], 16 * G)
                    with pe.Else():
                        pe.reg_add(due[b][g], due[b][g], 16)
                        for s in range(1, G - 1):
                            with pe.If(n > G * g + s):
                                pe.reg_add(due[b][g], due[b][g], 16)
                    pe.wait_ge(s_gat[b][g], pe.snap(due[b][g], min_val=16, max_val=16 * G * (PAIRS + 1)))
                    pe.wait_ge(s_gelu, t * NG + g + 1)
                    pe.matmul(z_ps[g % 2][:], ident[:],
                              slot[:, b, G * g:G * g + G, :].rearrange("p s d -> p (s d)"), start=True, stop=False)
                    pe.matmul(z_ps[g % 2][:].rearrange("p (s d) -> p s d", s=G), h_now[:, b, :], w_s4,
                              start=False, stop=True).then_inc(s_z, 1)

                def sum_of(g):
                    pe.wait_ge(s_prod, t * NG + g + 1)
                    for s in range(G * g, G * g + G):
                        pe.matmul(agg_ps[b][:, 0:P], slot[:, b, s, :], ident[:], start=False, stop=False)

                def group(g):
                    z_of(g)
                    if g >= 2:
                        sum_of(g - 2)
                    if g == NG - 1:
                        sum_of(g - 1)
                        sum_of(g)

                def skip(g):
                    pe.wait_ge(s_z, t * NG + g)
                    pe.sem_inc(s_z, NG - g)
                    for before in range(max(g - 2, 0), g):
                        sum_of(before)

                groups(pe, n, group, skip)
                pe.matmul(agg_ps[b][:, 0:P], zeros[:], zeros[:], start=False, stop=True).then_inc(s_agg, 1)

            due = [[pe.alloc_register(f"due{b}_{g}") for g in range(NG)] for b in range(2)]
            for b in range(2):
                for g in range(NG):
                    pe.reg_mov(due[b][g], 0)
            def transposes(q):
                pe.wait_ge(s_h, q + 1)
                if q >= 2:
                    pe.wait_ge(s_hT, q - 1)
                for j in range(4):
                    last = pe.transpose(z_ps[q % 2][:, j * P:(j + 1) * P], h[:, (4 * q + j) * D:(4 * q + j + 1) * D],
                                        ident[:])
                last.then_inc(s_hTp, 1)

            transposes(0)
            for q in range(Q):
                if q + 1 < Q:
                    transposes(q + 1)
                if q == 0:
                    stats(0, True)
                pe.wait_ge(s_hT, q + 1)
                if q >= 4:
                    pe.wait_ge(s_drc, q - 3)
                for j in range(4):
                    last = pe.matmul(d_ps[q % 4][:, j * D:(j + 1) * D], hT[:, (4 * q + j) * P:(4 * q + j + 1) * P],
                                     w_dT[:], start=True, stop=True)
                last.then_inc(s_dr, 1)
                if q == min(Q, 4) - 1:
                    stats(1, True)
            with pe.Fori(0, Q) as q:
                pe.wait_ge(s_dTc, q + 1)
                pe.matmul(work_ps[1][:], w_dT[:], hT[:, ds(q * QD, QD)], start=True, stop=True).then_inc(s_dT, 1)
            pe.wait_ge(s_drc, Q)
            with pe.Fori(0, VP - 1) as k:
                for b in range(2):
                    tile_sums(2 * k + b, b)
                    stats(2 * k + b + 2, True)
            with pe.Fori(VP - 1, PAIRS - 1) as k:
                for b in range(2):
                    tile_sums(2 * k + b, b)
                    stats(2 * k + b + 2)
            tile_sums(NT - 3, 0)
            stats(NT - 1)
            tile_sums(NT - 2, 1)
            tile_sums(NT - 1, 0)

            pe.wait_ge(s_dn, 1)
            n = pe.value_load(dense_n[0:1, 0:1], min_val=0, max_val=N)

            def dense_s(c, in_list):
                hold(s_dlist, c + 1)
                for j in range(8):
                    with pe.If(in_list(j)):
                        i = pe.value_load(row8_i[0:1, j:j + 1], min_val=0, max_val=N - 1)
                        pe.wait_ge(s_dscc, c * 8 + j + (2 if j == 0 else 1))
                        pe.matmul(work_ps[j % 2][:, 0:1], w_sT[:], hT[:, ds(i, 1)],
                                  start=True, stop=True).then_inc(s_dsc, 1)

            dense_rounds(pe, n, dense_s)


            def of_h(q):
                pe.matmul(up_ps[q % UP][:], w_hT[:], hT[:, q * QD:(q + 1) * QD], start=True, stop=False)

            def of_agg(q):
                pe.matmul(up_ps[q % UP][:], w_aT[:], aggT[:, q * QD:(q + 1) * QD], start=False, stop=True)\
                    .then_inc(s_up, 1)

            pe.wait_ge(s_aggc, NT + 2)
            pe.wait_ge(s_gelu, NT * NG + 2)
            for q in range(min(Q, UP)):
                of_h(q)
            pe.wait_ge(s_end, 1)
            of_agg(0)
            for q in range(Q):
                if q + 1 < Q:
                    of_agg(q + 1)
                pe.wait_ge(s_upg, q + 1)
                if q >= 2:
                    pe.wait_ge(s_hadd, q - 1)
                for j in range(4):
                    last = pe.transpose(new_ps[q % 2][:, j * P:(j + 1) * P], new_T[q % 2][:, j * P:(j + 1) * P],
                                        ident[:])
                last.then_inc(s_newT, 1)
                if q + UP < Q:
                    of_h(q + UP)

        @block.vector
        def _(dve):
            hold = holder(dve, s_held["dve"])
            dve.sem_inc(s_col, 2)
            dve.sem_inc(s_dco, 1)
            dve.sem_inc(s_dsum, 2)
            dve.memset(zeros[:], 0.0)
            dve.memset(sort_hi[:], 0)
            dve.memset(sort_lo[:], 0)
            dve.wait_ge(s_const, 7)
            dve.tensor_scalar(seg_code[:], iota_c, 16, VALID, ALU.logical_shift_left, ALU.bitwise_or)
            dve.tensor_scalar(iota_p, iota_p, PARTS - 1, 20, ALU.bitwise_and, ALU.logical_shift_left)\
                .then_inc(s_cdve, 1)
            dve.wait_ge(s_cdve, 1)
            dve.tensor_tensor(part_code[:], seg_code[:], iota_p, ALU.bitwise_or).then_inc(s_cdve, 1)

            def norm_stats(src, s_in, first, step, arrived=None, early=0):
                for t in range(early, T):
                    if arrived and t % 4 == 0:
                        dve.wait_ge(arrived[t // 4], 16)
                    last = dve.bn_stats(stats6[:, t, :], src[:, t * D:(t + 1) * D])
                last.then_inc(step, 1)
                dve.wait_ge(step, 1)
                for t in range(T):
                    last = dve.bn_aggr(mean_var[:, t, :], stats6[:, t, :])
                last.then_inc(s_cdve, 1)
                dve.wait_ge(s_cdve, first)
                dve.tensor_scalar(mean_var[:, :, 1], mean_var[:, :, 1], EPS, None, ALU.add).then_inc(step, 1)
                dve.wait_ge(s_std, s_in)
                dve.reciprocal(rstd[:], std[:]).then_inc(step, 1)
                dve.wait_ge(step, 3)
                dve.scalar_tensor_tensor(shift[:], mean_var[:, :, 0], -1.0, rstd[:], ALU.mult, ALU.mult)\
                    .then_inc(step, 1)

            norm_stats(x_sb, 1, 3, s_ln, s_x)
            dve.wait_ge(s_wT, 1)
            for j, w in enumerate((w_sT, w_dT, w_hT, w_aT)):
                last = dve.tensor_copy(w[:], z_ps[0][:, j * D:(j + 1) * D])
            last.then_inc(s_wTc, 1)

            def add_bias(q):
                dve.wait_ge(s_rows, 80)
                dve.wait_ge(s_dr, q + 1)
                dve.tensor_tensor(d_rows[:, q * QD:(q + 1) * QD].rearrange("p (t d) -> p t d", d=D),
                                  d_ps[q % 4][:].rearrange("p (t d) -> p t d", d=D), row4(msgb_row), ALU.add)\
                    .then_inc(s_drc, 1)

            def segments(b, parts):
                return adj_sb[:, b, 0:PW if parts else N].rearrange("p (c s) -> p s c", s=SEG)

            def find_values(u, k, b, parts=False):
                hold(s_adj[b], loaded(k, parts))
                seg = segments(b, parts)
                for s in range(SEG):
                    last = dve.max(vals[:, b, 8 * s:8 * s + 8], seg[:, s, :])
                last.then_inc(s_val, 1)

            def find_columns(u, b, parts=False):
                done = lambda n: dve.wait_ge(s_find, 3 * u + n)
                seg = segments(b, parts)
                hold(s_val, u + 1)
                for s in range(SEG):
                    last = dve.max_index(cols[:, 8 * s:8 * s + 8], vals[:, b, 8 * s:8 * s + 8], seg[:, s, :])
                last.then_inc(s_col, 1)
                dve.tensor_reduce(seg_full[:], vals[:, b, :].rearrange("p (s e) -> p s e", e=8)[:, :, 7], AX_X, ALU.max)
                dve.tensor_scalar(used[:], vals[:, b, :], 0.0, None, ALU.not_equal, ALU.add, accum_out=n_used[:])\
                    .then_inc(s_find, 1)
                dve.wait_ge(s_col, u + 3)
                dve.scalar_tensor_tensor(code[:, b, :], cols[:], 23 if parts else 20,
                                         (part_code if parts else seg_code)[:].bitcast(u32),
                                         ALU.logical_shift_left, ALU.bitwise_or)
                done(1)
                dve.wait_ge(s_neg, u + 3)
                dve.scalar_tensor_tensor(why1[:], seg_full[:], 0.0, neg[:, b:b + 1], ALU.not_equal, ALU.add)\
                    .then_inc(s_find, 1)
                done(2)
                dve.scalar_tensor_tensor(why2[:], n_used[:], float(SLOTS), why1[:], ALU.is_gt, ALU.add)\
                    .then_inc(s_find, 1)
                done(3)
                if not (isinstance(u, int) and u == 0):
                    dve.wait_ge(s_statT, u)
                dve.scalar_tensor_tensor(row_stat[:, 0:1], why2[:], 0.0, n_used[:], ALU.is_equal, ALU.mult)
                dve.tensor_scalar(row_stat[:, 1:2], why2[:], 0.0, None, ALU.not_equal).then_inc(s_stat, 1)

            def sort(u, b):
                done = lambda n: dve.wait_ge(s_key, 4 * u + n)
                dve.wait_ge(s_statT, u + 1)
                dve.wait_ge(s_iss, u + 1)
                dve.wait_ge(s_aggc, u + 1)
                dve.tensor_scalar(row_ok[:], or_ps, 0.0, None, ALU.is_equal).then_inc(s_key, 1)
                dve.tensor_reduce(longest[0:1, b:b + 1], stat_ps[0:1, 0:P], AX_X, ALU.max)
                dve.tensor_copy(dense_flag[0:1, ds(u * P, P)], stat_ps[0:1, P:2 * P]).then_inc(s_cnt, 1)
                done(1)
                dve.tensor_scalar(kept[:], vals[:, b, :], row_ok[:, 0:1], None, ALU.mult).then_inc(s_key, 1)
                done(2)
                dve.scalar_tensor_tensor(code_kept[:].bitcast(fp32), kept[:], 0.0, code[:, b, :].bitcast(fp32),
                                         ALU.not_equal, ALU.mult).then_inc(s_key, 1)
                done(3)
                dve.scalar_tensor_tensor(key_hi[:], kept[:].bitcast(u32), 16, code_kept[:],
                                         ALU.logical_shift_right, ALU.bitwise_or).then_inc(s_hi, 1)
                dve.scalar_tensor_tensor(key_lo[:], kept[:].bitcast(u32), HALF, code_kept[:],
                                         ALU.bitwise_and, ALU.bitwise_or).then_inc(s_lo, 1)
                hold(s_cnt, u + 1)
                n = dve.value_load(longest[0:1, b:b + 1], min_val=0, max_val=SLOTS)
                f_hi, f_lo = key_hi[:].bitcast(fp32), key_lo[:].bitcast(fp32)
                t_hi, t_lo = sort_hi[:].bitcast(fp32), sort_lo[:].bitcast(fp32)
                per = 2 * RANKS + 1

                def rank(r):
                    at = slice(8 * r, 8 * r + 8)
                    hold(s_hi, per * u + 2 * r + 1)
                    dve.max(t_hi[:, at], f_hi).then_inc(s_hi, 1)
                    hold(s_lo, per * u + 2 * r + 1)
                    dve.max(t_lo[:, at], f_lo).then_inc(s_lo, 1)
                    hold(s_hi, per * u + 2 * r + 2)
                    dve.match_replace(f_hi, t_hi[:, at], f_hi, 0.0).then_inc(s_hi, 1)
                    hold(s_lo, per * u + 2 * r + 2)
                    dve.match_replace(f_lo, t_lo[:, at], f_lo, 0.0).then_inc(s_lo, 1)

                for r in range(SURE):
                    rank(r)
                with dve.If(n > 8 * SURE):
                    rank(SURE)
                    for r in range(SURE + 1, RANKS):
                        with dve.If(n > 8 * r):
                            rank(r)
                        with dve.Else():
                            dve.wait_ge(s_hi, per * u + 2 * r + 1)
                            dve.sem_inc(s_hi, 2)
                            dve.wait_ge(s_lo, per * u + 2 * r + 1)
                            dve.sem_inc(s_lo, 2)
                    dve.nop()
                with dve.Else():
                    dve.wait_ge(s_hi, per * u + 2 * SURE + 1)
                    dve.sem_inc(s_hi, 2 * (RANKS - SURE))
                    dve.wait_ge(s_lo, per * u + 2 * SURE + 1)
                    dve.sem_inc(s_lo, 2 * (RANKS - SURE))
                dve.wait_ge(s_hi, per * u + per)
                dve.tensor_scalar(idx[:, b, :].bitcast(u32), sort_hi[:], 16, 0xFFF,
                                  ALU.logical_shift_right, ALU.bitwise_and).then_inc(s_idx, 1)
                dve.tensor_scalar(val_hi[:], sort_hi[:], HALF, 16, ALU.bitwise_and, ALU.logical_shift_left)\
                    .then_inc(s_key, 1)
                done(4)
                dve.wait_ge(s_lo, per * u + per)
                dve.scalar_tensor_tensor(val[:, b, :], sort_lo[:], HALF, val_hi[:],
                                         ALU.bitwise_and, ALU.bitwise_or).then_inc(s_lst, 1)

            for b in range(2):
                find_values(b, 0, b, True)
                find_columns(b, b, True)
            for q in range(Q):
                add_bias(q)
                if q == min(Q, 4) - 1:
                    sort(0, 0)
            with dve.Fori(0, VP - 1) as k:
                for b in range(2):
                    find_values(2 * k + b + 2, k + 1, b, True)
                    sort(2 * k + b + 1, 1 - b)
                    find_columns(2 * k + b + 2, b, True)
            with dve.Fori(VP - 1, PAIRS - 1) as k:
                for b in range(2):
                    find_values(2 * k + b + 2, k + 1, b)
                    sort(2 * k + b + 1, 1 - b)
                    find_columns(2 * k + b + 2, b)
            find_values(NT - 1, PAIRS, 0)
            sort(NT - 2, 1)
            find_columns(NT - 1, 0)
            sort(NT - 1, 0)
            dve.wait_ge(s_cnt, NT)
            with nc.allow_low_precision("flags of 0 and 1, and their count"):
                dve.tensor_reduce(first_flag[:], dense_flag[0:1, 0:PARTS * P].rearrange("a (r q) -> a r q", q=PARTS),
                                  AX_X, ALU.max).then_inc(s_cdve, 1)
                dve.tensor_reduce(aggT[:, 0:P], agg_parts[:].rearrange("p (r q) -> p r q", q=PARTS), AX_X, ALU.add)
                dve.wait_ge(s_cdve, 4)
                rows_flag = dense_flag[0:1, (PARTS - 1) * P:NT * P]
                dve.tensor_copy(rows_flag[:, 0:P], first_flag[:]).then_inc(s_cdve, 1)
                dve.wait_ge(s_cdve, 5)
                dve.tensor_reduce(dense_n[:], rows_flag, AX_X, ALU.add).then_inc(s_dn, 1)

            def list_rows(c):
                dve.wait_ge(s_dstep, c * 2 + 2)
                dve.tensor_scalar(row8_i[:], key8[:], -1.0, 0.0, ALU.add, ALU.max).then_inc(s_dlist, 1)

            dve.wait_ge(s_nld, 16)
            dve.tensor_tensor(dense_key, rows_flag, dense_key, ALU.mult).then_inc(s_dstep, 1)
            hold(s_dstep, 1)
            dve.max(key8[:], dense_key).then_inc(s_dstep, 1)
            list_rows(0)
            hold(s_dn, 1)

            def dense_sums(c, in_list):
                hold(s_dlist, c + 1)
                with dve.If(in_list(8)):
                    hold(s_dstep, c * 2 + 2)
                    dve.match_replace(dense_key, key8[:], dense_key, 0.0).then_inc(s_dstep, 1)
                    hold(s_dstep, c * 2 + 3)
                    dve.max(key8[:], dense_key).then_inc(s_dstep, 1)
                for j in range(8):
                    with dve.If(in_list(j)):
                        i = dve.value_load(row8_i[0:1, j:j + 1], min_val=0, max_val=N - 1)
                        dve.wait_ge(s_dg, c * 8 + j + 1)
                        per_round = len(range(j % 3, 8, 3))
                        dve.wait_ge(s_drow[j % 3], c * 16 * per_round + 16 * (j // 3 + 1))
                        dve.tensor_tensor_reduce(out=g_row[j % 2], in0=g_row[j % 2],
                                                 in1=dense_adj[j % 3], scale=1.0, scalar=0.0,
                                                 op0=ALU.mult, op1=ALU.add,
                                                 accum_out=dense_sum[:, j:j + 1]).then_inc(s_dsum, 1)
                        dve.wait_ge(s_dsum, c * 8 + j + 3)
                        dve.tensor_copy(aggT[:, ds(i, 1)], dense_sum[:, j:j + 1]).then_inc(s_dco, 1)

                with dve.If(in_list(8)):
                    dve.wait_ge(s_dco, c * 8 + 9)
                    list_rows(c + 1)

            n = dve.value_load(dense_n[0:1, 0:1], min_val=0, max_val=N)
            dense_rounds(dve, n, dense_sums)
            hold(s_dco, n + 1)
            dve.sem_inc(s_end, 1)

            for q in range(Q):
                dve.wait_ge(s_newT, q + 1)
                dve.tensor_tensor(f_sb[:, q * QD:(q + 1) * QD], new_ps[q % 2][:], h[:, q * QD:(q + 1) * QD],
                                  ALU.add).then_inc(s_hadd, 1)
                if q:
                    dve.wait_ge(s_hadd, q)
                    for t in range(4 * q - 4, 4 * q):
                        dve.bn_stats(stats6[:, t, :], f_sb[:, t * D:(t + 1) * D])
            dve.wait_ge(s_hadd, Q)
            norm_stats(f_sb, 2, 6, s_fin, early=T - 4)
            dve.wait_ge(s_xb, Q)
            with dve.Fori(0, Q) as q:
                dve.wait_ge(s_nrm, q + 1)
                dve.tensor_tensor(quad(f_sb, q), quad(f_sb, q), row4(lnw_row), ALU.mult).then_inc(s_scl, 1)
                dve.wait_ge(s_scl, q + 1)
                dve.tensor_tensor(quad(f_sb, q), quad(f_sb, q), quad(x_sb, q), ALU.add).then_inc(s_y, 1)


_INS = ["x", "adj", "L0_gnn_msg_w", "L0_gnn_msg_b", "L0_gnn_upd_w", "L0_gnn_upd_b", "L0_gnn_ln_w", "L0_gnn_ln_b"]


def kernel(**inputs):
    import numpy as _np
    import concourse.bacc as _bacc
    from concourse import mybir as _mybir
    from concourse.bass_utils import run_bass_kernel_spmd as _run

    nc = _bacc.Bacc("TRN2", target_bir_lowering=False, num_devices=1)
    arrays, args = {}, []
    for name in _INS:
        a = _np.ascontiguousarray(inputs[name])
        arrays[f"in_{name}"] = a
        args.append(nc.dram_tensor(f"in_{name}", a.shape, _mybir.dt.from_np(a.dtype), kind="ExternalInput").ap())
    shape = arrays["in_x"].shape
    args.append(nc.dram_tensor("out_0", shape, _mybir.dt.float32, kind="ExternalOutput").ap())
    gnn_sparse_rows_kernel(nc, *args)
    r = _run(nc, [arrays], core_ids=[0])
    return r.results[0]["out_0"]
```
